# Optimizing a Trainium2 kernel written in Bass

```python
import numpy as np
import jax
import jax.numpy as jnp

def _softmax(x, axis=-1):
    return jax.nn.softmax(x, axis=axis)

def _gelu(x):
    return jax.nn.gelu(x, approximate=True)

def _silu(x):
    return jax.nn.silu(x)

def _sigmoid(x):
    return jax.nn.sigmoid(x)

def _layernorm(x, axis=-1, eps=1e-05):
    m = jnp.mean(x, axis=axis, keepdims=True)
    v = jnp.var(x, axis=axis, keepdims=True)
    return (x - m) / jnp.sqrt(v + eps)

def _scatter_add(tgt, idx, src, axis=0):
    return tgt.at[idx].add(src)

def _segment_sum(src, seg, n):
    return jax.ops.segment_sum(src, seg, n)
kernel_name = 'mk_pixart_seq_d2_seqx_r4_fd9828'

def setup_inputs(seed: int=0):
    np.random.seed(seed)
    _w = jnp.asarray

    def _rec_inputs():
        import jax
        import jax.numpy as jnp
        _rk = jax.random.key(seed)
        x = 7.22e-05 + 1 * jax.random.normal(jax.random.fold_in(_rk, 1), (4, 1024, 256), jnp.float32)
        _lenS = 1024 - jax.random.randint(jax.random.fold_in(_rk, 7), (4,), 0, max(1, 1024 // 4) + 1, jnp.int32)
        _lenS2 = 77 - jax.random.randint(jax.random.fold_in(_rk, 8), (4,), 0, max(1, 77 // 4) + 1, jnp.int32)
        cond_1024 = 0.000887014 + 1.03683 * jax.random.normal(jax.random.fold_in(_rk, 11), (4, 256), jnp.float32)
        _ctx_1024P = jax.random.normal(jax.random.fold_in(_rk, 12), (4, 16, 256), jnp.float32)
        _ctx_1024c = jax.random.dirichlet(jax.random.fold_in(_rk, 512), 0.3 * jnp.ones((16,), jnp.float32), (4, 77))
        _ctx_1024t = jnp.einsum('bsk,bkd->bsd', _ctx_1024c, _ctx_1024P)
        _ctx_1024t = _ctx_1024t * jax.lax.rsqrt(jnp.mean(jnp.square(_ctx_1024t)) + 1e-12) * 0.953939
        ctx_1024 = 0.00086875 + 0.999764 * (_ctx_1024t + 0.3 * jax.random.normal(jax.random.fold_in(_rk, 612), (4, 77, 256), jnp.float32))
        return (x, cond_1024, ctx_1024)
    x, cond_1024, ctx_1024 = _rec_inputs()

    def _L0_xcond_setup():
        import jax, jax.numpy as jnp
        import numpy as np
        C = 256
        H = 16
        D = C // H
        WIN = 128
        SHIFT = 64
        TOPK = 16
        HID = 1024
        EPS = 1e-06

        def _ln(x):
            x32 = x.astype(jnp.float32)
            m = x32.mean(-1, keepdims=True)
            v = jnp.mean((x32 - m) ** 2, axis=-1, keepdims=True)
            return ((x32 - m) * jax.lax.rsqrt(v + EPS)).astype(x.dtype)

        def _self_attn(h, w_qkv, b_qkv, w_so, b_so):
            B, L, _ = h.shape
            qkv = h @ w_qkv + b_qkv
            qkv = jnp.roll(qkv, -SHIFT, axis=1)
            nw = L // WIN
            qkv = qkv.reshape(B, nw, WIN, 3, H, D)
            q, k, v = (qkv[:, :, :, 0], qkv[:, :, :, 1], qkv[:, :, :, 2])
            scores = jnp.einsum('bnqhd,bnkhd->bnhqk', q, k) / jnp.sqrt(jnp.float32(D)).astype(h.dtype)
            attn = jax.nn.softmax(scores, axis=-1)
            o = jnp.einsum('bnhqk,bnkhd->bnqhd', attn, v).reshape(B, L, C)
            o = jnp.roll(o, SHIFT, axis=1)
            return o @ w_so + b_so

        def _topk_cross_attn(h, ctx, w_q, b_q, w_kv, b_kv, w_co, b_co):
            B, L, _ = h.shape
            Lc = ctx.shape[1]
            q = (h @ w_q + b_q).reshape(B, L, H, D)
            kv = (ctx @ w_kv + b_kv).reshape(B, Lc, 2, H, D)
            k, v = (kv[:, :, 0], kv[:, :, 1])
            scores = jnp.einsum('bqhd,bkhd->bhqk', q, k) / jnp.sqrt(jnp.float32(D)).astype(h.dtype)
            top_s, top_i = jax.lax.top_k(scores, TOPK)
            attn = jax.nn.softmax(top_s, axis=-1)
            v_bh = jnp.transpose(v, (0, 2, 1, 3))
            vg = jnp.take_along_axis(v_bh[:, :, None, :, :], top_i[..., None], axis=3)
            o = jnp.einsum('bhqk,bhqkd->bqhd', attn, vg).reshape(B, L, C)
            return o @ w_co + b_co

        def _swiglu(h, w_m1, b_m1, w_m2, b_m2):
            u = h @ w_m1 + b_m1
            a, b = (u[..., :HID], u[..., HID:])
            return jax.nn.silu(a) * b @ w_m2 + b_m2
        key = jax.random.key(seed)
        ks = jax.random.split(key, 24)
        s = 0.02
        inp = {'x': jax.random.normal(ks[0], (2, 1024, C), jnp.float32), 'mod': jax.random.normal(ks[1], (2, C), jnp.float32), 'context': jax.random.normal(ks[2], (2, 256, C), jnp.float32), 'w_ada': jax.random.normal(ks[3], (C, 9 * C), jnp.float32) * s, 'b_ada': jnp.zeros((9 * C,), jnp.float32), 'w_qkv': jax.random.normal(ks[4], (C, 3 * C), jnp.float32) * s, 'b_qkv': jnp.zeros((3 * C,), jnp.float32), 'w_so': jax.random.normal(ks[5], (C, C), jnp.float32) * s, 'b_so': jnp.zeros((C,), jnp.float32), 'w_q': jax.random.normal(ks[6], (C, C), jnp.float32) * s, 'b_q': jnp.zeros((C,), jnp.float32), 'w_kv': jax.random.normal(ks[7], (C, 2 * C), jnp.float32) * s, 'b_kv': jnp.zeros((2 * C,), jnp.float32), 'w_co': jax.random.normal(ks[8], (C, C), jnp.float32) * s, 'b_co': jnp.zeros((C,), jnp.float32), 'w_m1': jax.random.normal(ks[9], (C, 2 * HID), jnp.float32) * s, 'b_m1': jnp.zeros((2 * HID,), jnp.float32), 'w_m2': jax.random.normal(ks[10], (HID, C), jnp.float32) * s, 'b_m2': jnp.zeros((C,), jnp.float32)}
        return inp
    _L0_xcond_all = _L0_xcond_setup()
    _L0_xcond_in = {k: v for k, v in _L0_xcond_all.items() if k in ('w_ada', 'b_ada', 'w_qkv', 'b_qkv', 'w_so', 'b_so', 'w_q', 'b_q', 'w_kv', 'b_kv', 'w_co', 'b_co', 'w_m1', 'b_m1', 'w_m2', 'b_m2')}
    del _L0_xcond_all

    def _L1_xcond_setup():
        import jax, jax.numpy as jnp
        import numpy as np
        EPS = 1e-05

        def _ada_ln(x, c, W_ss, b_ss):
            mu = jnp.mean(x, axis=-1, keepdims=True)
            var = jnp.mean((x - mu) ** 2, axis=-1, keepdims=True)
            h = (x - mu) / jnp.sqrt(var + EPS)
            ss = jax.nn.silu(c) @ W_ss + b_ss
            scale, bias = jnp.split(ss, 2, axis=-1)
            return (1.0 + scale)[:, None, :] * h + bias[:, None, :]
        key = jax.random.key(seed)
        ks = jax.random.split(key, 12)
        B, Lq, Lkv, H = (8, 512, 128, 256)
        s = 0.02
        return {'x_q': jax.random.normal(ks[0], (B, Lq, H), jnp.float32), 'x_kv': jax.random.normal(ks[1], (B, Lkv, H), jnp.float32), 't_vec': jax.random.normal(ks[2], (B, H), jnp.float32), 'Wq': jax.random.normal(ks[3], (H, H), jnp.float32) * s, 'bq': jnp.zeros((H,), jnp.float32), 'Wkv': jax.random.normal(ks[4], (H, 2 * H), jnp.float32) * s, 'bkv': jnp.zeros((2 * H,), jnp.float32), 'Wp': jax.random.normal(ks[5], (H, H), jnp.float32) * s, 'bp': jnp.zeros((H,), jnp.float32), 'Wss_q': jax.random.normal(ks[6], (H, 2 * H), jnp.float32) * s, 'bss_q': jnp.zeros((2 * H,), jnp.float32), 'Wss_kv': jax.random.normal(ks[7], (H, 2 * H), jnp.float32) * s, 'bss_kv': jnp.zeros((2 * H,), jnp.float32)}
    _L1_xcond_all = _L1_xcond_setup()
    _L1_xcond_in = {k: v for k, v in _L1_xcond_all.items() if k in ('Wq', 'bq', 'Wkv', 'bkv', 'Wp', 'bp', 'Wss_q', 'bss_q', 'Wss_kv', 'bss_kv')}
    del _L1_xcond_all
    return {'x': x, 'cond_1024': cond_1024, 'ctx_1024': ctx_1024, 'L0_xcond_w_ada': _L0_xcond_in['w_ada'], 'L0_xcond_b_ada': _L0_xcond_in['b_ada'], 'L0_xcond_w_qkv': _L0_xcond_in['w_qkv'], 'L0_xcond_b_qkv': _L0_xcond_in['b_qkv'], 'L0_xcond_w_so': _L0_xcond_in['w_so'], 'L0_xcond_b_so': _L0_xcond_in['b_so'], 'L0_xcond_w_q': _L0_xcond_in['w_q'], 'L0_xcond_b_q': _L0_xcond_in['b_q'], 'L0_xcond_w_kv': _L0_xcond_in['w_kv'], 'L0_xcond_b_kv': _L0_xcond_in['b_kv'], 'L0_xcond_w_co': _L0_xcond_in['w_co'], 'L0_xcond_b_co': _L0_xcond_in['b_co'], 'L0_xcond_w_m1': _L0_xcond_in['w_m1'], 'L0_xcond_b_m1': _L0_xcond_in['b_m1'], 'L0_xcond_w_m2': _L0_xcond_in['w_m2'], 'L0_xcond_b_m2': _L0_xcond_in['b_m2'], 'L1_xcond_Wq': _L1_xcond_in['Wq'], 'L1_xcond_bq': _L1_xcond_in['bq'], 'L1_xcond_Wkv': _L1_xcond_in['Wkv'], 'L1_xcond_bkv': _L1_xcond_in['bkv'], 'L1_xcond_Wp': _L1_xcond_in['Wp'], 'L1_xcond_bp': _L1_xcond_in['bp'], 'L1_xcond_Wss_q': _L1_xcond_in['Wss_q'], 'L1_xcond_bss_q': _L1_xcond_in['bss_q'], 'L1_xcond_Wss_kv': _L1_xcond_in['Wss_kv'], 'L1_xcond_bss_kv': _L1_xcond_in['bss_kv']}

def reference(x, cond_1024, ctx_1024, L0_xcond_w_ada, L0_xcond_b_ada, L0_xcond_w_qkv, L0_xcond_b_qkv, L0_xcond_w_so, L0_xcond_b_so, L0_xcond_w_q, L0_xcond_b_q, L0_xcond_w_kv, L0_xcond_b_kv, L0_xcond_w_co, L0_xcond_b_co, L0_xcond_w_m1, L0_xcond_b_m1, L0_xcond_w_m2, L0_xcond_b_m2, L1_xcond_Wq, L1_xcond_bq, L1_xcond_Wkv, L1_xcond_bkv, L1_xcond_Wp, L1_xcond_bp, L1_xcond_Wss_q, L1_xcond_bss_q, L1_xcond_Wss_kv, L1_xcond_bss_kv):
    import jax
    import jax.numpy as jnp

    def _L0_xcond_ref(x, mod, context, w_ada, b_ada, w_qkv, b_qkv, w_so, b_so, w_q, b_q, w_kv, b_kv, w_co, b_co, w_m1, b_m1, w_m2, b_m2):
        import jax, jax.numpy as jnp
        import numpy as np
        C = 256
        H = 16
        D = C // H
        WIN = 128
        SHIFT = 64
        TOPK = 16
        HID = 1024
        EPS = 1e-06

        def _ln(x):
            x32 = x.astype(jnp.float32)
            m = x32.mean(-1, keepdims=True)
            v = jnp.mean((x32 - m) ** 2, axis=-1, keepdims=True)
            return ((x32 - m) * jax.lax.rsqrt(v + EPS)).astype(x.dtype)

        def _self_attn(h, w_qkv, b_qkv, w_so, b_so):
            B, L, _ = h.shape
            qkv = h @ w_qkv + b_qkv
            qkv = jnp.roll(qkv, -SHIFT, axis=1)
            nw = L // WIN
            qkv = qkv.reshape(B, nw, WIN, 3, H, D)
            q, k, v = (qkv[:, :, :, 0], qkv[:, :, :, 1], qkv[:, :, :, 2])
            scores = jnp.einsum('bnqhd,bnkhd->bnhqk', q, k) / jnp.sqrt(jnp.float32(D)).astype(h.dtype)
            attn = jax.nn.softmax(scores, axis=-1)
            o = jnp.einsum('bnhqk,bnkhd->bnqhd', attn, v).reshape(B, L, C)
            o = jnp.roll(o, SHIFT, axis=1)
            return o @ w_so + b_so

        def _topk_cross_attn(h, ctx, w_q, b_q, w_kv, b_kv, w_co, b_co):
            B, L, _ = h.shape
            Lc = ctx.shape[1]
            q = (h @ w_q + b_q).reshape(B, L, H, D)
            kv = (ctx @ w_kv + b_kv).reshape(B, Lc, 2, H, D)
            k, v = (kv[:, :, 0], kv[:, :, 1])
            scores = jnp.einsum('bqhd,bkhd->bhqk', q, k) / jnp.sqrt(jnp.float32(D)).astype(h.dtype)
            top_s, top_i = jax.lax.top_k(scores, TOPK)
            attn = jax.nn.softmax(top_s, axis=-1)
            v_bh = jnp.transpose(v, (0, 2, 1, 3))
            vg = jnp.take_along_axis(v_bh[:, :, None, :, :], top_i[..., None], axis=3)
            o = jnp.einsum('bhqk,bhqkd->bqhd', attn, vg).reshape(B, L, C)
            return o @ w_co + b_co

        def _swiglu(h, w_m1, b_m1, w_m2, b_m2):
            u = h @ w_m1 + b_m1
            a, b = (u[..., :HID], u[..., HID:])
            return jax.nn.silu(a) * b @ w_m2 + b_m2
        m = jax.nn.silu(mod) @ w_ada + b_ada
        sh_msa, sc_msa, g_msa, sh_mca, sc_mca, g_mca, sh_mlp, sc_mlp, g_mlp = [m[:, i * C:(i + 1) * C][:, None, :] for i in range(9)]
        h = _ln(x) * (1 + sc_msa) + sh_msa
        h = _self_attn(h, w_qkv, b_qkv, w_so, b_so)
        x = x + h * g_msa
        h = _ln(x) * (1 + sc_mca) + sh_mca
        h = _topk_cross_attn(h, context, w_q, b_q, w_kv, b_kv, w_co, b_co)
        x = x + h * g_mca
        h = _ln(x) * (1 + sc_mlp) + sh_mlp
        h = _swiglu(h, w_m1, b_m1, w_m2, b_m2)
        x = x + h * g_mlp
        return x

    def _L1_xcond_ref(x_q, x_kv, t_vec, Wq, bq, Wkv, bkv, Wp, bp, Wss_q, bss_q, Wss_kv, bss_kv):
        import jax, jax.numpy as jnp
        import numpy as np
        EPS = 1e-05

        def _ada_ln(x, c, W_ss, b_ss):
            mu = jnp.mean(x, axis=-1, keepdims=True)
            var = jnp.mean((x - mu) ** 2, axis=-1, keepdims=True)
            h = (x - mu) / jnp.sqrt(var + EPS)
            ss = jax.nn.silu(c) @ W_ss + b_ss
            scale, bias = jnp.split(ss, 2, axis=-1)
            return (1.0 + scale)[:, None, :] * h + bias[:, None, :]
        B, Lq, H = x_q.shape
        Lkv = x_kv.shape[1]
        nh = 16
        dh = H // nh
        xq = _ada_ln(x_q, t_vec, Wss_q, bss_q)
        xkv = _ada_ln(x_kv, t_vec, Wss_kv, bss_kv)
        q = (xq @ Wq + bq).reshape(B, Lq, nh, dh)
        kv = (xkv @ Wkv + bkv).reshape(B, Lkv, 2, nh, dh)
        k = kv[:, :, 0]
        v = kv[:, :, 1]
        scores = jnp.einsum('bqhd,bkhd->bhqk', q, k) / jnp.sqrt(jnp.float32(dh))
        attn = jax.nn.softmax(scores, axis=-1)
        out = jnp.einsum('bhqk,bkhd->bqhd', attn, v).reshape(B, Lq, H)
        return x_q + (out @ Wp + bp)
    x = _L0_xcond_ref(x, cond_1024, ctx_1024, L0_xcond_w_ada, L0_xcond_b_ada, L0_xcond_w_qkv, L0_xcond_b_qkv, L0_xcond_w_so, L0_xcond_b_so, L0_xcond_w_q, L0_xcond_b_q, L0_xcond_w_kv, L0_xcond_b_kv, L0_xcond_w_co, L0_xcond_b_co, L0_xcond_w_m1, L0_xcond_b_m1, L0_xcond_w_m2, L0_xcond_b_m2)
    x = _L1_xcond_ref(x, ctx_1024, cond_1024, L1_xcond_Wq, L1_xcond_bq, L1_xcond_Wkv, L1_xcond_bkv, L1_xcond_Wp, L1_xcond_bp, L1_xcond_Wss_q, L1_xcond_bss_q, L1_xcond_Wss_kv, L1_xcond_bss_kv)
    return x

_drawn_inputs = setup_inputs


def setup_inputs(seed=0):
    import zlib

    import numpy as np

    out = dict(_drawn_inputs(seed))
    spreads = {'L0_xcond_b_ada': (0.0, 0.397),
     'L0_xcond_b_qkv': (0.0, 0.8),
     'L0_xcond_b_so': (0.0, 0.375),
     'L0_xcond_b_q': (0.0, 0.8),
     'L0_xcond_b_kv': (0.0, 0.8),
     'L0_xcond_b_co': (0.0, 0.396),
     'L0_xcond_b_m1': (0.0, 0.8),
     'L0_xcond_b_m2': (0.0, 1.426),
     'L1_xcond_bq': (0.0, 2.0),
     'L1_xcond_bkv': (0.0, 0.8),
     'L1_xcond_bp': (0.0, 0.638),
     'L1_xcond_bss_q': (0.0, 2.0),
     'L1_xcond_bss_kv': (0.0, 2.0)}
    factors = {'L0_xcond_w_qkv': 8.0,
     'L0_xcond_w_so': 6.101,
     'L0_xcond_w_q': 7.343,
     'L0_xcond_w_kv': 3.878,
     'L0_xcond_w_co': 3.486,
     'L0_xcond_w_m1': 6.127,
     'L0_xcond_w_m2': 6.11,
     'L1_xcond_Wq': 54.179,
     'L1_xcond_Wss_q': 61.553,
     'L1_xcond_Wkv': 3.826,
     'L1_xcond_Wp': 3.792,
     'L1_xcond_Wss_kv': 8.0}
    for name, (base, spread) in spreads.items():
        noise = np.random.default_rng([zlib.crc32(name.encode()), seed]).standard_normal(out[name].shape)
        drawn = base * np.exp(spread * noise) if base else spread * noise
        out[name] = jnp.asarray(drawn.astype(out[name].dtype))
    for name, factor in factors.items():
        out[name] = (out[name] * factor).astype(out[name].dtype)
    return out
```

```python
from contextlib import ExitStack

import numpy as np
import concourse.bass as bass
from concourse import mybir

F32 = mybir.dt.float32
ALU = mybir.AluOpType
ACT = mybir.ActivationFunctionType
AX = mybir.AxisListType

BATCH, LEN, CH, HEADS, LC = 4, 1024, 256, 16, 77
P = 128
HD = CH // HEADS
KC = CH // P
HH = HEADS // KC
TPB = LEN // P
TILES = BATCH * TPB
SHIFT, TOPK, HID = 64, 16, 1024
HJ = HID // P
PAIRS = HEADS * LC
NCH = -(-PAIRS // P)
TAIL = PAIRS - (NCH - 1) * P
V1 = HD + 1
H0 = [P * c // LC for c in range(NCH)]
NH = [min(P * c + P - 1, PAIRS - 1) // LC - H0[c] + 1 for c in range(NCH)]
NHM = max(NH)
SCALE = 1.0 / float(HD) ** 0.5
LOW = -3.0e38
EPS0, EPS1 = 1e-6, 1e-5

COLS = [("mod_scale", 10), ("mod_shift", 10), ("bq_a", 2), ("bk_a", 2), ("bv_a", 2), ("bq_b", 2), ("bk_b", 2),
        ("bv_b", 2), ("bq_d", 2), ("bk_d", 2), ("bv_d", 2), ("bm1_a", HJ), ("bm1_b", HJ)]
COL = {}
for _name, _n in COLS:
    COL[_name] = sum(n for k, n in COLS[:len(COL)])
NCOLS = sum(n for _, n in COLS)


def block_kernel(nc, a, out):
    ctx = ExitStack()
    with ctx:
        def sb(name, shape, dt=F32, stack=ctx):
            return stack.enter_context(nc.sbuf_tensor(name, shape, dt))

        def sem(name):
            return ctx.enter_context(nc.semaphore(name))

        ps = ctx.enter_context(nc.psum_tensor("ps", [P, 8, 512], F32))
        PS = {s: ps[:, 2 * n:2 * n + 2, :] for n, s in enumerate("ABCD")}
        scratch = {s: nc.dram_tensor(f"v_flat_{s}", [BATCH, HEADS, LC, HD], F32, kind="Internal").ap() for s in "BD"}

        w_qkv = sb("w_qkv_sb", [P, KC, 3 * CH])
        w_so = sb("w_so_sb", [P, KC, CH])
        w_q = sb("w_q_sb", [P, KC, CH])
        w_co = sb("w_co_sb", [P, KC, CH])
        w_m1 = sb("w_m1_sb", [P, KC, 2 * HID])
        w_m2 = sb("w_m2_sb", [P, HJ, CH])
        w_qd = sb("w_qd_sb", [P, KC, CH])
        w_pd = sb("w_pd_sb", [P, KC, CH])
        cols = sb("cols_sb", [P, NCOLS])
        ident = sb("ident_sb", [P, P])
        mask4 = sb("mask4_sb", [P, 4])
        scaleT = sb("scaleT", [P, 10, BATCH])
        shiftT = sb("shiftT", [P, 10, BATCH])
        gate = sb("gate", [P, 3, BATCH, CH])
        gate_b = sb("gate_b", [P, 3, BATCH, CH])
        bp_row = sb("bp_row", [P, CH])
        kT = {s: sb(f"kT_{s}", [P, KC, BATCH, LC]) for s in "BD"}
        vblk = {s: sb(f"vblk_{s}", [P, BATCH, NCH, NHM * V1]) for s in "BD"}
        half_neg = sb("half_neg", [P, BATCH])

        eps = sb("eps", [P, 2])
        carrier = sb("carrier", [P, 2])

        X, XN, XG, HT, TMP, ST, MV, VE, RS = ({} for _ in range(9))

        def work(s):
            X[s] = sb(f"x_{s}", [P, CH])
            XN[s] = sb(f"xn_{s}", [P, CH])
            XG[s] = sb(f"xg_{s}", [P, CH])
            HT[s] = sb(f"hT_{s}", [P, KC, P])
            TMP[s] = sb(f"tmp_{s}", [P, CH])
            ST[s] = sb(f"st_{s}", [P, 6])
            MV[s] = sb(f"mv_{s}", [P, 2])
            VE[s] = sb(f"ve_{s}", [P, 1])
            RS[s] = sb(f"rstd_{s}", [P, 1])

        QT, KB, PR, PT, O, OT, MX, RC = ({} for _ in range(8))

        def attention_work(s, pairs):
            QT[s] = sb(f"qT_{s}", [P, KC, P])
            KB[s] = sb(f"kblk_{s}", [P, KC, 4, pairs])
            O[s] = sb(f"o_{s}", [P, HEADS, HD])
            OT[s] = sb(f"oT_{s}", [P, KC, P])
            MX[s] = sb(f"mx_{s}", [P, HEADS, 8])
            RC[s] = sb(f"rc_{s}", [P, HEADS, 1])
            if pairs == P:
                PR[s] = sb(f"p_{s}", [P, HEADS, P])
                PT[s] = sb(f"pT_{s}", [P, HEADS, P])
            else:
                PR[s] = sb(f"p_{s}", [P, NCH * P])
                PT[s] = sb(f"pT_{s}", [P, NCH, P])

        work("A")
        attention_work("A", P)
        kTa = sb("kT_A", [P, KC, P])
        va = sb("v_A", [P, HEADS, V1])

        with ExitStack() as early:
            w_mod = sb("w_mod_sb", [P, KC, 10 * CH], F32, early)
            w_gate = sb("w_gate_sb", [P, KC, 3 * CH], F32, early)
            w_kv = {s: sb(f"w_kv_{s}_sb", [P, KC, 2 * CH], F32, early) for s in "BD"}
            rows = sb("rows_sb", [P, 6, CH], F32, early)
            condT = sb("condT_sb", [P, KC, BATCH], F32, early)
            scT = sb("scT", [P, KC, BATCH], F32, early)
            screp = sb("screp", [P, KC, BATCH, P], F32, early)
            ctxT = sb("ctxT_sb", [P, KC, BATCH, LC], F32, early)
            ctxn = sb("ctx_sb", [LC, BATCH, CH], F32, early)
            cn = sb("ctx_norm", [LC, BATCH, CH], F32, early)
            kvT = sb("kvT", [P, KC, BATCH, LC], F32, early)
            cst = sb("ctx_st", [LC, BATCH, 6], F32, early)
            cmv = sb("ctx_mv", [LC, BATCH, 2], F32, early)
            cve = sb("ctx_ve", [LC, BATCH], F32, early)
            crs = sb("ctx_rstd", [LC, BATCH], F32, early)
            vn = {s: sb(f"v_nat_{s}", [LC, BATCH, CH], F32, early) for s in "BD"}
            vf = {s: sb(f"v_flat_sb_{s}", [P, BATCH, NCH, V1], F32, early) for s in "BD"}
            vmask = sb("vmask_sb", [P, NCH, NHM], F32, early)

        work("B")
        attention_work("B", LC)
        S = sb("scores_B", [P, HEADS, LC])
        R = sb("scores_left_B", [P, HEADS, LC])
        MX2 = sb("mx2_B", [P, HEADS, 8])
        work("C")
        SA = sb("silu_C", [P, HJ, P])
        G = sb("hidden_C", [P, HJ, P])
        work("D")
        attention_work("D", LC)
        Y = sb("y_D", [P, CH])

        ld = {n: sem(f"ld_{n}") for n in ("small", "mod", "gate", "qkv", "so", "b", "kv_b", "kv_d", "c", "d", "ctx")}
        silu_done, rep_done = sem("silu_done"), sem("rep_done")
        mod_ps, mod_done, gate_ps, gate_done, gb_done = (sem(n) for n in (
            "mod_ps", "mod_done", "gate_ps", "gate_done", "gb_done"))
        zeroed = sem("zeroed")
        cstat, crstd, cnorm, ct_ps, kv_hT = (sem(n) for n in ("cstat", "crstd", "cnorm", "ct_ps", "kv_hT"))
        ck_ps, ck_done, cv_ps, cv_done, v_out, v_in, vb_done = (
            {s: sem(f"{n}_{s}") for s in "BD"} for n in ("ck_ps", "ck_done", "cv_ps", "cv_done", "v_out", "v_in", "vb_done"))
        pool_self, dve_self = sem("pool_self"), sem("dve_self")

        def per_stage(name, stages="ABCD"):
            return {s: sem(f"{name}_{s}") for s in stages}

        x_in = per_stage("x_in")
        stats = per_stage("stats")
        rstd = per_stage("rstd")
        xn_ok = per_stage("xn_ok")
        xg_ok = per_stage("xg_ok")
        h_ps = per_stage("h_ps")
        h_ok = per_stage("h_ok")
        q_ps = per_stage("q_ps", "ABD")
        q_ok = per_stage("q_ok", "ABD")
        kb_ok = per_stage("kb_ok", "ABD")
        s_ps = per_stage("s_ps", "ABD")
        s_rd = per_stage("s_rd", "ABD")
        mx_ok = per_stage("mx_ok", "AD")
        p_ok = per_stage("p_ok", "ABD")
        pt_ps = per_stage("pt_ps", "ABD")
        pt_ok = per_stage("pt_ok", "ABD")
        pv_ps = per_stage("pv_ps", "ABD")
        rc_ok = per_stage("rc_ok", "ABD")
        o_ok = per_stage("o_ok", "ABD")
        ot_ps = per_stage("ot_ps", "ABD")
        ot_ok = per_stage("ot_ok", "ABD")
        y_ps = per_stage("y_ps")
        tmp_ok = per_stage("tmp_ok")
        top_ok = sem("top_ok")
        sm_ok = sem("sm_ok")
        e_ok = sem("e_ok")
        u_ps, sa_ok, g_ok = sem("u_ps"), sem("sa_ok"), sem("g_ok")
        y_out = sem("y_out")

        NEXT = {"A": "B", "B": "C", "C": "D"}
        LN = {"A": 0, "B": 1, "C": 2, "D": 3}
        LAG = {"A": 0, "B": 1, "C": 2, "D": 3}
        EPS = {"A": EPS0, "B": EPS0, "C": EPS0, "D": EPS1}
        BQ = {"A": "bq_a", "B": "bq_b", "D": "bq_d"}
        BV = {"A": "bv_a", "B": "bv_b", "D": "bv_d"}
        WO = {"A": w_so, "B": w_co, "D": w_pd}

        def col(name, n=0):
            return cols[:, COL[name] + n:COL[name] + n + 1]

        def pick(view, t):
            b = t // TPB
            return view[:, b, :] if isinstance(b, int) else view[:, bass.ds(b, 1), :].rearrange("p b n -> p (b n)")

        def mod_col(table, idx, t):
            return pick(table[:, idx, :].rearrange("p (b n) -> p b n", n=1), t)

        def iterate(engine, body):
            for i in range(4):
                body({s: i - LAG[s] for s in "ABCD" if i >= LAG[s]})
            with engine.Fori(4, TILES) as i:
                body({s: i - LAG[s] for s in "ABCD"})
            for i in range(TILES, TILES + 3):
                body({s: i - LAG[s] for s in "ABCD" if i - LAG[s] < TILES})

        def settle(dve, semaphore, value):
            dve.wait_ge(semaphore, value)
            if not isinstance(value, int):
                nc.vector.tensor_copy(carrier[:, 1:2], carrier[:, 0:1])

        def first(t):
            return isinstance(t, int) and t == 0

        def pairs_view(ap, c):
            return ap[:, c * HH * LC:(c + 1) * HH * LC].rearrange("p (h k) -> p h k", h=HH)

        def score_banks(s, c=None):
            return PS[s][:, :, 0:4 * LC]

        block = ctx.enter_context(nc.Block())

        @block.sync
        def _(sp):
            def load(dst, src, s):
                sp.dma_start(dst, src).then_inc(ld[s], 16)

            x_blocks = a["x"].rearrange("b (u p) c -> (b u) p c", p=SHIFT)
            out_blocks = out.rearrange("b (u p) c -> (b u) p c", p=SHIFT)
            PER = LEN // SHIFT

            def halves(t):
                second = (t // TPB) * PER + (2 * t + 2) % PER
                return 2 * t + 1, second

            def block_of(view, u):
                return view[u] if isinstance(u, int) else view[bass.ds(u, 1)].rearrange("a p c -> (a p) c")

            def load_x(t):
                if not first(t):
                    sp.wait_ge(xn_ok["A"], t)
                    sp.wait_ge(xg_ok["A"], t)
                for n, u in enumerate(halves(t)):
                    sp.dma_start(X["A"][n * SHIFT:(n + 1) * SHIFT, :], block_of(x_blocks, u)).then_inc(x_in["A"], 16)

            def store_y(t):
                sp.wait_ge(tmp_ok["D"], t + 1)
                for n, u in enumerate(halves(t)):
                    sp.dma_start(block_of(out_blocks, u), Y[n * SHIFT:(n + 1) * SHIFT, :]).then_inc(y_out, 16)

            load(condT[:], a["condT"], "small")
            load(cols[:], a["cols"], "small")
            load(rows[:], a["rows"][:, 0:6, :].partition_broadcast(P).rearrange("p a n c -> p (a n) c"), "small")
            load(ident[:], a["ident"], "small")
            load(mask4[:], a["mask4"], "small")
            load(w_mod[:, 0, :], a["w_mod"][:, 0, :], "mod")
            load(w_mod[:, 1, :], a["w_mod"][:, 1, :], "mod")
            load_x(0)
            load(w_qkv[:], a["w_qkv"], "qkv")
            load(w_gate[:], a["w_gate"], "gate")
            load(w_so[:], a["w_so"], "so")
            load(w_kv["B"][:], a["w_kv"], "kv_b")
            load(w_kv["D"][:], a["Wkv"], "kv_d")
            load(w_q[:], a["w_q"], "b")
            load(w_co[:], a["w_co"], "b")
            load(w_m1[:], a["w_m1"], "c")
            load(w_m2[:], a["w_m2"], "c")
            load(w_qd[:], a["Wq"], "d")
            load(w_pd[:], a["Wp"], "d")

            def body(tile):
                if "A" in tile:
                    t = tile["A"] + 1
                    if not (isinstance(t, int) and t == TILES):
                        load_x(t)
                if "D" in tile:
                    store_y(tile["D"])

            for i in range(4):
                body({s: i - LAG[s] for s in "ABCD" if i >= LAG[s]})
            with sp.Fori(4, TILES - 1) as i:
                body({s: i - LAG[s] for s in "ABCD"})
            for i in range(TILES - 1, TILES + 3):
                body({s: i - LAG[s] for s in "ABCD" if i - LAG[s] < TILES})
            sp.wait_ge(y_out, 32 * TILES)

        @block.gpsimd
        def _(pool):
            g = nc.gpsimd
            selfs = [0]

            def link(ins):
                selfs[0] += 1
                ins.then_inc(pool_self, 1)
                pool.wait_ge(pool_self, selfs[0])

            g.dma_start(ctxn[:], a["ctxn"]).then_inc(ld["ctx"], 16)
            g.dma_start(ctxT[:], a["ctxT"]).then_inc(ld["ctx"], 16)
            g.dma_start(vmask[:], a["vmask"]).then_inc(ld["ctx"], 16)
            g.dma_start(bp_row[:], a["rows"][:, 6, :].partition_broadcast(P).rearrange("p a c -> p (a c)")).then_inc(ld["ctx"], 16)
            g.memset(half_neg[:], -0.5).then_inc(zeroed, 1)
            g.memset(va[:, :, HD:V1], 1.0).then_inc(zeroed, 1)
            for s in "BD":
                link(g.memset(vf[s][:], 0.0))
                g.memset(vf[s][:, :, :, HD:V1], 1.0).then_inc(zeroed, 1)
            g.memset(carrier[:], 0.0).then_inc(zeroed, 1)
            g.memset(eps[:, 0:1], EPS0).then_inc(zeroed, 1)
            g.memset(eps[:, 1:2], EPS1).then_inc(zeroed, 1)
            pool.wait_ge(zeroed, 7)

            def setup_gates():
                pool.wait_ge(gate_done, 1)
                pool.wait_ge(ld["small"], 16 * 5)
                for n in range(3):
                    ins = g.tensor_tensor(gate_b[:, n], gate[:, n], rows[:, 3 + n:4 + n, :].to_broadcast([P, BATCH, CH]), ALU.mult)
                ins.then_inc(gb_done, 1)
                pool.wait_ge(gb_done, 1)

            def setup_context_rstd():
                pool.wait_ge(cstat, 2 * BATCH)
                link(g.tensor_scalar(cve[:], cmv[:, :, 1], EPS1, None, ALU.add))
                g.tensor_tensor(crs[:], cve[:], half_neg[0:LC, :], ALU.pow).then_inc(crstd, 1)

            def setup_flat(s):
                pool.wait_ge(cv_done[s], 1)
                for b in range(BATCH):
                    g.dma_start(scratch[s][b].rearrange("h k d -> k h d"),
                                vn[s][:, b, :].rearrange("k (h d) -> k h d", h=HEADS)).then_inc(v_out[s], 16)
                pool.wait_ge(v_out[s], 16 * BATCH)
                full = (NCH - 1) * P
                for b in range(BATCH):
                    flat = scratch[s][b].rearrange("h k d -> (h k) d")
                    g.dma_start(vf[s][:, b, 0:NCH - 1, 0:HD],
                                flat[0:full].rearrange("(c p) d -> p c d", p=P)).then_inc(v_in[s], 16)
                    g.dma_start(vf[s][0:TAIL, b, NCH - 1, 0:HD], flat[full:PAIRS]).then_inc(v_in[s], 16)

            def setup_blocks(s):
                pool.wait_ge(v_in[s], 32 * BATCH)
                pool.wait_ge(ld["ctx"], 16 * 4)
                for b in range(BATCH):
                    ins = g.tensor_tensor(vblk[s][:, b].rearrange("p c (n v) -> p c n v", n=NHM),
                                          vf[s][:, b].unsqueeze(2).to_broadcast([P, NCH, NHM, V1]),
                                          vmask[:].unsqueeze(3).to_broadcast([P, NCH, NHM, V1]), ALU.mult)
                ins.then_inc(vb_done[s], 1)

            def reciprocal_root(s, t):
                pool.wait_ge(stats[s], 2 * t + 2)
                g.tensor_tensor(VE[s][:], MV[s][:, 1:2], eps[:, LN[s] // 3:LN[s] // 3 + 1], ALU.add).then_inc(rstd[s], 1)
                pool.wait_ge(rstd[s], 2 * t + 1)
                g.tensor_tensor(RS[s][:], VE[s][:], half_neg[:, 0:1], ALU.pow).then_inc(rstd[s], 1)

            def gated_bias(s, t):
                if s == "A":
                    pool.wait_ge(x_in[s], 32 * t + 32)
                if s != "D" and not first(t):
                    pool.wait_ge(x_in[NEXT[s]], t)
                if s == "D":
                    if not first(t):
                        pool.wait_ge(tmp_ok["D"], t)
                    bias = bp_row[:]
                    pool.wait_ge(x_in[s], t + 1)
                else:
                    bias = pick(gate_b[:, LN[s]], t)
                    if s != "A":
                        pool.wait_ge(x_in[s], t + 1)
                g.tensor_tensor(XG[s][:], X[s][:], bias, ALU.add).then_inc(xg_ok[s], 1)

            def key_blocks(s, t):
                if s == "A":
                    pool.wait_ge(q_ok[s], t + 1)
                else:
                    pool.wait_ge(ck_done[s], 1)
                    if not first(t):
                        pool.wait_ge(s_ps[s], 2 * t)
                for c in range(KC):
                    if s == "A":
                        keys = kTa[:, c, :]
                        n = P
                    else:
                        keys = pick(kT[s][:, c], t)
                        n = LC
                    ins = g.tensor_tensor(KB[s][:, c], keys.unsqueeze(1).to_broadcast([P, 4, n]),
                                          mask4[:].unsqueeze(2).to_broadcast([P, 4, n]), ALU.mult)
                ins.then_inc(kb_ok[s], 1)

            def less_max(t, c):
                pool.wait_ge(top_ok, 8 * t + 4 * c + 1)
                g.tensor_tensor(pairs_view(PR["B"], c), S[:, c * HH:(c + 1) * HH, :],
                                MX["B"][:, c * HH:(c + 1) * HH, 0:1].to_broadcast([P, HH, LC]),
                                ALU.subtract).then_inc(sm_ok, 1)

            def residual(s, t):
                pool.wait_ge(tmp_ok[s], t + 1)
                nxt = NEXT[s]
                pool.wait_ge(xg_ok[s], t + 1)
                if not first(t):
                    pool.wait_ge(xn_ok[nxt], t)
                    pool.wait_ge(xg_ok[nxt], t)
                g.tensor_tensor(X[nxt][:], XG[s][:], TMP[s][:], ALU.add).then_inc(x_in[nxt], 1)

            def body(tile):
                for s in "BDCA":
                    if s in tile:
                        reciprocal_root(s, tile[s])
                        gated_bias(s, tile[s])
                for s in "BD":
                    if s in tile:
                        key_blocks(s, tile[s])
                if "A" in tile:
                    key_blocks("A", tile["A"])
                for c in range(KC):
                    if "B" in tile:
                        less_max(tile["B"], c)
                for s in "CAB":
                    if s in tile:
                        residual(s, tile[s])

            setup_gates()
            setup_context_rstd()
            setup_flat("B")
            setup_blocks("B")
            setup_flat("D")
            setup_blocks("D")
            g.memset(PR["B"][:, PAIRS:NCH * P], 0.0).then_inc(zeroed, 1)
            g.memset(PR["D"][:, PAIRS:NCH * P], 0.0).then_inc(zeroed, 1)
            iterate(pool, body)

        @block.scalar
        def _(act):
            sc = nc.scalar

            def setup():
                act.wait_ge(ld["small"], 16 * 5)
                sc.activation(scT[:], condT[:], ACT.Silu).then_inc(silu_done, 1)
                act.wait_ge(ck_ps["B"], 1)
                for c in range(KC):
                    ins = sc.activation(kT["B"][:, c].rearrange("p b k -> p (b k)"), PS["A"][:, c, 0:BATCH * LC],
                                        ACT.Identity, bias=col("bk_b", c))
                ins.then_inc(ck_done["B"], 1)
                act.wait_ge(cv_ps["B"], 1)
                sc.copy(vn["B"][:].rearrange("k (m n) c -> k m (n c)", m=2), PS["B"][0:LC]).then_inc(cv_done["B"], 1)
                act.wait_ge(ct_ps, 1)
                act.wait_ge(mod_done, 1)
                for c in range(KC):
                    for b in range(BATCH):
                        ins = sc.activation(kvT[:, c, b, :], PS["C"][:, c, b * LC:(b + 1) * LC], ACT.Identity,
                                            scale=scaleT[:, 8 + c, b:b + 1], bias=shiftT[:, 8 + c, b:b + 1])
                ins.then_inc(kv_hT, 1)
                act.wait_ge(ck_ps["D"], 1)
                for c in range(KC):
                    ins = sc.activation(kT["D"][:, c].rearrange("p b k -> p (b k)"), PS["A"][:, c, 0:BATCH * LC],
                                        ACT.Identity, bias=col("bk_d", c))
                ins.then_inc(ck_done["D"], 1)
                act.wait_ge(cv_ps["D"], 1)
                sc.copy(vn["D"][:].rearrange("k (m n) c -> k m (n c)", m=2), PS["D"][0:LC]).then_inc(cv_done["D"], 1)

            def modulate(s, t):
                act.wait_ge(h_ps[s], t + 1)
                for c in range(KC):
                    ins = sc.activation(HT[s][:, c, :], PS[s][:, 1, c * P:(c + 1) * P], ACT.Identity,
                                        scale=mod_col(scaleT, 2 * LN[s] + c, t), bias=mod_col(shiftT, 2 * LN[s] + c, t))
                ins.then_inc(h_ok[s], 1)

            def queries(s, t):
                act.wait_ge(q_ps[s], t + 1)
                for c in range(KC):
                    ins = sc.activation(QT[s][:, c, :], PS[s][:, 0, c * P:(c + 1) * P], ACT.Identity, bias=col(BQ[s], c))
                if s == "A":
                    for c in range(KC):
                        sc.activation(kTa[:, c, :], PS[s][:, 0, (KC + c) * P:(KC + c + 1) * P], ACT.Identity,
                                      bias=col("bk_a", c))
                    ins = sc.copy(va[:, :, 0:HD], PS[s][:, 1, CH:2 * CH].rearrange("p (h d) -> p h d", h=HEADS))
                ins.then_inc(q_ok[s], 1)

            def exponentials(s, t, c):
                if s == "A":
                    act.wait_ge(s_rd[s], 2 * t + c + 1)
                    w = PR[s][:, c * HH:(c + 1) * HH, :]
                    sc.activation(w, w, ACT.Exp, scale=SCALE).then_inc(p_ok[s], 1)
                elif s == "B":
                    act.wait_ge(sm_ok, 2 * t + c + 1)
                    w = pairs_view(PR[s], c)
                    sc.activation(w, w, ACT.Exp, scale=SCALE).then_inc(e_ok, 1)
                else:
                    act.wait_ge(s_rd[s], 2 * t + c + 1)
                    w = pairs_view(PR[s], c)
                    sc.activation(w, w, ACT.Exp, scale=SCALE).then_inc(p_ok[s], 1)

            def copy_scores(t, c):
                act.wait_ge(s_ps["B"], 2 * t + c + 1)
                sc.copy(S[:, c * HH:(c + 1) * HH, :].rearrange("p (j h) k -> p j (h k)", j=2),
                        score_banks("B")).then_inc(s_rd["B"], 1)

            def weights_out(s, t, c):
                act.wait_ge(pt_ps[s], 2 * t + c + 1)
                if s == "A":
                    ins = sc.copy(PT[s][:, c * HH:(c + 1) * HH, :].rearrange("p (j h) q -> p j (h q)", j=2), PS[s])
                elif c == 0:
                    ins = sc.copy(PT[s][:, 0:4, :].rearrange("p c q -> p (c q)"), PS[s][:, 0, :])
                else:
                    sc.copy(PT[s][:, 4:8, :].rearrange("p c q -> p (c q)"), PS[s][:, 1, :])
                    ins = sc.copy(PT[s][:, 8:NCH, :].rearrange("p c q -> p (c q)"), PS[s][:, 0, 0:(NCH - 8) * P])
                ins.then_inc(pt_ok[s], 1)

            def output_t(s, t):
                act.wait_ge(ot_ps[s], t + 1)
                for c in range(KC):
                    ins = sc.activation(OT[s][:, c, :], PS[s][:, 1, c * P:(c + 1) * P], ACT.Identity, bias=col(BV[s], c))
                ins.then_inc(ot_ok[s], 1)

            def silu(t, j):
                act.wait_ge(u_ps, HJ * t + j + 1)
                sc.activation(SA[:, j, :], PS["C"][:, j % 2, 0:P], ACT.Silu, bias=col("bm1_a", j)).then_inc(sa_ok, 1)

            def body(tile):
                def run(step, s, *more):
                    if s in tile:
                        step(s, tile[s], *more)
                run(modulate, "A"); run(modulate, "B"); run(modulate, "D"); run(modulate, "C")
                run(queries, "B"); run(queries, "A"); run(queries, "D")
                if "B" in tile:
                    copy_scores(tile["B"], 0)
                run(exponentials, "A", 0)
                run(exponentials, "D", 0)
                if "B" in tile:
                    copy_scores(tile["B"], 1)
                run(exponentials, "A", 1)
                run(exponentials, "D", 1)
                for j in range(HJ):
                    if "C" in tile:
                        silu(tile["C"], j)
                run(weights_out, "A", 0); run(weights_out, "D", 0)
                run(weights_out, "A", 1); run(weights_out, "D", 1)
                run(exponentials, "B", 0); run(exponentials, "B", 1)
                run(weights_out, "B", 0)
                run(output_t, "A"); run(output_t, "D")
                run(weights_out, "B", 1)
                run(output_t, "B")

            setup()
            iterate(act, body)

        @block.vector
        def _(dve):
            v = nc.vector

            def setup():
                dve.wait_ge(silu_done, 1)
                for c in range(KC):
                    ins = v.tensor_copy(screp[:, c], scT[:, c, :].unsqueeze(2).to_broadcast([P, BATCH, P]))
                ins.then_inc(rep_done, 1)
                dve.wait_ge(ld["ctx"], 16 * 4)
                for b in range(BATCH):
                    ins = v.bn_stats(cst[:, b, :], ctxn[:, b, :]).then_inc(cstat, 1)
                dve.wait_ge(cstat, BATCH)
                for b in range(BATCH):
                    v.bn_aggr(cmv[:, b, :], cst[:, b, :]).then_inc(cstat, 1)
                dve.wait_ge(mod_ps, 1)
                dve.wait_ge(ld["small"], 16 * 5)
                mod = PS["A"][:, 0, 0:80].rearrange("p (m i b) -> p m i b", m=2, b=BATCH)
                v.scalar_tensor_tensor(out=scaleT[:], in0=mod[:, 0], scalar=1.0,
                                       in1=cols[:, COL["mod_scale"]:COL["mod_scale"] + 10].unsqueeze(2).to_broadcast(
                                           [P, 10, BATCH]), op0=ALU.add, op1=ALU.add)
                v.tensor_tensor(shiftT[:], mod[:, 1], cols[:, COL["mod_shift"]:COL["mod_shift"] + 10].unsqueeze(2)
                                .to_broadcast([P, 10, BATCH]), ALU.add).then_inc(mod_done, 1)
                dve.wait_ge(gate_ps, 1)
                for n in range(3):
                    ins = v.tensor_tensor(gate[:, n].rearrange("p (m b) c -> p m b c", m=2),
                                          ps[:, 2 + 2 * n:4 + 2 * n, :].rearrange("p m (b c) -> p m b c", b=2),
                                          rows[:, n:n + 1, :].unsqueeze(1).to_broadcast([P, 2, 2, CH]), ALU.add)
                ins.then_inc(gate_done, 1)
                dve.wait_ge(crstd, 1)
                for b in range(BATCH):
                    ins = v.tensor_scalar(cn[:, b, :], ctxn[:, b, :], cmv[:, b, 0:1], crs[:, b:b + 1],
                                          ALU.subtract, ALU.mult)
                ins.then_inc(cnorm, 1)

            def statistics(s, t):
                dve.wait_ge(x_in[s], 32 * t + 32 if s == "A" else t + 1)
                v.bn_stats(ST[s][:], X[s][:]).then_inc(stats[s], 1)
                if not first(t):
                    dve.wait_ge(xn_ok[s], t)
                settle(dve, stats[s], 2 * t + 1)
                v.bn_aggr(MV[s][:], ST[s][:]).then_inc(stats[s], 1)

            def normalise(s, t):
                dve.wait_ge(rstd[s], 2 * t + 2)
                if not first(t):
                    dve.wait_ge(h_ps[s], t)
                v.tensor_scalar(XN[s][:], X[s][:], MV[s][:, 0:1], RS[s][:], ALU.subtract, ALU.mult).then_inc(xn_ok[s], 1)

            def maxima(s, t, c):
                dve.wait_ge(s_ps[s], 2 * t + c + 1)
                view = (PS[s].rearrange("p j (h k) -> p j h k", h=4) if s == "A"
                        else score_banks(s).rearrange("p j (h k) -> p j h k", h=4))
                v.tensor_reduce(MX[s][:, c * HH:(c + 1) * HH, 0].rearrange("p (j h) -> p j h", j=2), view,
                                AX.X, ALU.max).then_inc(mx_ok[s], 1)
                dve.wait_ge(mx_ok[s], 2 * t + c + 1)
                w = PR[s][:, c * HH:(c + 1) * HH, :] if s == "A" else pairs_view(PR[s], c)
                n = P if s == "A" else LC
                v.tensor_tensor(w.rearrange("p (j h) k -> p j h k", j=2), view,
                                MX[s][:, c * HH:(c + 1) * HH, 0:1].rearrange("p (j h) o -> p j h o", j=2)
                                .to_broadcast([P, 2, 4, n]), ALU.subtract).then_inc(s_rd[s], 1)

            def select(t, c):
                settle(dve, s_rd["B"], 2 * t + c + 1)
                heads = range(c * HH, (c + 1) * HH)
                k = 8 * t + 4 * c
                for h in heads:
                    ins = v.max(MX["B"][:, h, :], S[:, h, :])
                ins.then_inc(top_ok, 1)
                settle(dve, top_ok, k + 1)
                for h in heads:
                    ins = v.match_replace(R[:, h, :], MX["B"][:, h, :], S[:, h, :], LOW)
                ins.then_inc(top_ok, 1)
                settle(dve, top_ok, k + 2)
                for h in heads:
                    ins = v.max(MX2[:, h, :], R[:, h, :])
                ins.then_inc(top_ok, 1)
                settle(dve, top_ok, k + 3)
                for h in heads:
                    ins = v.match_replace(R[:, h, :], MX2[:, h, :], R[:, h, :], LOW)
                ins.then_inc(top_ok, 1)

            def keep_chosen(t, c):
                dve.wait_ge(top_ok, 8 * t + 4 * c + 4)
                dve.wait_ge(e_ok, 2 * t + c + 1)
                w = PR["B"][:, c * HH * LC:(c + 1) * HH * LC]
                v.scalar_tensor_tensor(out=w, in0=R[:, c * HH:(c + 1) * HH, :].rearrange("p h k -> p (h k)"), scalar=LOW,
                                       in1=w, op0=ALU.is_equal, op1=ALU.mult).then_inc(p_ok["B"], 1)

            def normalise_output(s, t):
                dve.wait_ge(pv_ps[s], t + 1)
                acc = PS[s][:, 0, 0:HEADS * V1].rearrange("p (h v) -> p h v", h=HEADS)
                v.reciprocal(RC[s][:], acc[:, :, HD:V1]).then_inc(rc_ok[s], 1)
                dve.wait_ge(rc_ok[s], t + 1)
                v.tensor_tensor(O[s][:], acc[:, :, 0:HD], RC[s][:].to_broadcast([P, HEADS, HD]),
                                ALU.mult).then_inc(o_ok[s], 1)

            def gated(s, t):
                dve.wait_ge(y_ps[s], t + 1)
                y = PS[s][:, 0, 0:CH]
                if s == "D":
                    dve.wait_ge(xg_ok[s], t + 1)
                    if not first(t):
                        dve.wait_ge(y_out, 32 * t)
                    v.tensor_tensor(Y[:], y, XG[s][:], ALU.add).then_inc(tmp_ok[s], 1)
                    return
                if first(t):
                    dve.wait_ge(gate_done, 1)
                else:
                    dve.wait_ge(x_in[NEXT[s]], t)
                v.tensor_tensor(TMP[s][:], y, pick(gate[:, LN[s]], t), ALU.mult).then_inc(tmp_ok[s], 1)

            def hidden(t, j):
                dve.wait_ge(sa_ok, HJ * t + j + 1)
                v.scalar_tensor_tensor(out=G[:, j, :], in0=PS["C"][:, j % 2, P:2 * P], scalar=col("bm1_b", j),
                                       in1=SA[:, j, :], op0=ALU.add, op1=ALU.mult).then_inc(g_ok, 1)

            def body(tile):
                def run(step, s, *more):
                    if s in tile:
                        step(s, tile[s], *more)
                for s in "BDCA":
                    run(statistics, s)
                for s in "BDCA":
                    run(normalise, s)
                run(maxima, "A", 0)
                run(maxima, "D", 0)
                run(maxima, "A", 1)
                run(maxima, "D", 1)
                if "B" in tile:
                    select(tile["B"], 0)
                for j in range(4):
                    if "C" in tile:
                        hidden(tile["C"], j)
                if "B" in tile:
                    select(tile["B"], 1)
                for j in range(4, HJ):
                    if "C" in tile:
                        hidden(tile["C"], j)
                if "B" in tile:
                    keep_chosen(tile["B"], 0)
                    keep_chosen(tile["B"], 1)
                run(normalise_output, "A"); run(normalise_output, "D")
                run(gated, "C"); run(gated, "A"); run(gated, "D")
                run(normalise_output, "B")
                run(gated, "B")

            setup()
            dve.wait_ge(zeroed, 7)
            iterate(dve, body)

        @block.tensor
        def _(pe):
            mm = nc.tensor.matmul

            def setup():
                pe.wait_ge(rep_done, 1)
                pe.wait_ge(ld["mod"], 32)
                for i in range(20):
                    for c in range(KC):
                        ins = mm(PS["A"][:, 0, i * BATCH:(i + 1) * BATCH], w_mod[:, c, i * P:(i + 1) * P], scT[:, c, :],
                                 start=(c == 0), stop=(c == KC - 1))
                ins.then_inc(mod_ps, 1)
                pe.wait_ge(ld["gate"], 16)
                for n in range(3):
                    for b in range(BATCH):
                        for c in range(KC):
                            ins = mm(ps[:, 2 + 2 * n + b // 2, (b % 2) * CH:(b % 2 + 1) * CH], screp[:, c, b, :],
                                     w_gate[:, c, n * CH:(n + 1) * CH], start=(c == 0), stop=(c == KC - 1))
                ins.then_inc(gate_ps, 1)
                pe.wait_ge(mod_done, 1)
                pe.wait_ge(ld["ctx"], 16 * 4)
                pe.wait_ge(ld["kv_b"], 16)
                context(ctxT, "B")
                pe.wait_ge(gate_done, 1)
                context_values(ctxT, "B")
                pe.wait_ge(cnorm, 1)
                pe.wait_ge(ld["small"], 16 * 5)
                for c in range(KC):
                    for b in range(BATCH):
                        ins = nc.tensor.transpose(PS["C"][:, c, b * LC:(b + 1) * LC], cn[:, b, c * P:(c + 1) * P],
                                                  ident[0:LC, 0:LC])
                ins.then_inc(ct_ps, 1)
                pe.wait_ge(kv_hT, 1)
                pe.wait_ge(ld["kv_d"], 16)
                pe.wait_ge(ck_done["B"], 1)
                context(kvT, "D")
                context_values(kvT, "D")
                pe.wait_ge(ck_done["D"], 1)
                pe.wait_ge(cv_done["B"], 1)
                pe.wait_ge(cv_done["D"], 1)

            def context(src, s):
                for c in range(KC):
                    for k in range(KC):
                        ins = mm(PS["A"][:, c, 0:BATCH * LC], w_kv[s][:, k, c * P:(c + 1) * P],
                                 src[:, k].rearrange("p b k -> p (b k)"), start=(k == 0), stop=(k == KC - 1))
                ins.then_inc(ck_ps[s], 1)

            def context_values(src, s):
                for b in range(BATCH):
                    for k in range(KC):
                        ins = mm(PS[s][0:LC, b // 2, (b % 2) * CH:(b % 2 + 1) * CH], src[:, k, b, :],
                                 w_kv[s][:, k, CH:2 * CH], start=(k == 0), stop=(k == KC - 1))
                ins.then_inc(cv_ps[s], 1)

            def transpose_h(s, t):
                pe.wait_ge(xn_ok[s], t + 1)
                for c in range(KC):
                    ins = nc.tensor.transpose(PS[s][:, 1, c * P:(c + 1) * P], XN[s][:, c * P:(c + 1) * P], ident[:])
                ins.then_inc(h_ps[s], 1)

            def project_q(s, t):
                pe.wait_ge(h_ok[s], t + 1)
                if first(t):
                    pe.wait_ge(ld[{"A": "qkv", "B": "b", "D": "d"}[s]], 32 if s != "A" else 16)
                else:
                    pe.wait_ge(tmp_ok[s], t)
                w = {"A": w_qkv, "B": w_q, "D": w_qd}[s]
                for c in range(4 if s == "A" else 2):
                    for k in range(KC):
                        ins = mm(PS[s][:, 0, c * P:(c + 1) * P], w[:, k, c * P:(c + 1) * P], HT[s][:, k, :],
                                 start=(k == 0), stop=(k == KC - 1))
                if s == "A":
                    for k in range(KC):
                        ins = mm(PS[s][:, 1, CH:2 * CH], HT[s][:, k, :], w[:, k, 2 * CH:3 * CH],
                                 start=(k == 0), stop=(k == KC - 1))
                ins.then_inc(q_ps[s], 1)

            def scores(s, t, c):
                if c == 0:
                    pe.wait_ge(q_ok[s], t + 1)
                    pe.wait_ge(kb_ok[s], t + 1)
                else:
                    pe.wait_ge(s_rd[s], 2 * t + 1)
                n = 4 * (P if s == "A" else LC)
                for j in range(2):
                    rows_ = slice(64 * j, 64 * j + 64)
                    ins = mm(PS[s][:, j, 0:n], QT[s][rows_, c, :], KB[s][rows_, c].rearrange("p h k -> p (h k)"),
                             start=True, stop=True)
                ins.then_inc(s_ps[s], 1)

            def transpose_p(s, t, c):
                if c == 0:
                    pe.wait_ge(s_rd[s], 2 * t + 2)
                    if s != "A" and first(t):
                        pe.wait_ge(zeroed, 9)
                else:
                    pe.wait_ge(pt_ok[s], 2 * t + 1)
                pe.wait_ge(p_ok[s], 2 * t + c + 1)
                if s == "A":
                    for h in range(HH):
                        ins = nc.tensor.transpose(PS[s][:, h // 4, (h % 4) * P:(h % 4 + 1) * P],
                                                  PR[s][:, c * HH + h, :], ident[:])
                else:
                    for n in (range(4) if c == 0 else range(4, NCH)):
                        bank = 1 if 4 <= n < 8 else 0
                        ins = nc.tensor.transpose(PS[s][:, bank, (n % 4) * P:(n % 4 + 1) * P],
                                                  PR[s][:, n * P:(n + 1) * P], ident[:])
                ins.then_inc(pt_ps[s], 1)

            def weigh_values(s, t):
                pe.wait_ge(pt_ok[s], 2 * t + 2)
                if s == "A":
                    for h in range(HEADS):
                        ins = mm(PS[s][:, 0, h * V1:(h + 1) * V1], PT[s][:, h, :], va[:, h, :], start=True, stop=True)
                else:
                    if first(t):
                        pe.wait_ge(vb_done[s], 1)
                    for n in range(NCH):
                        ins = mm(PS[s][:, 0, H0[n] * V1:(H0[n] + NH[n]) * V1], PT[s][:, n, :],
                                 pick(vblk[s][:, :, n, 0:NH[n] * V1], t), start=(n == 0), stop=(n == NCH - 1),
                                 skip_group_check=True)
                ins.then_inc(pv_ps[s], 1)

            def transpose_o(s, t):
                pe.wait_ge(o_ok[s], t + 1)
                for c in range(KC):
                    ins = nc.tensor.transpose(PS[s][:, 1, c * P:(c + 1) * P],
                                              O[s][:].rearrange("p h d -> p (h d)")[:, c * P:(c + 1) * P], ident[:])
                ins.then_inc(ot_ps[s], 1)

            def project_o(s, t):
                pe.wait_ge(ot_ok[s], t + 1)
                if first(t) and s == "A":
                    pe.wait_ge(ld["so"], 16)
                for k in range(KC):
                    ins = mm(PS[s][:, 0, 0:CH], OT[s][:, k, :], WO[s][:, k, :], start=(k == 0), stop=(k == KC - 1))
                ins.then_inc(y_ps[s], 1)

            def up(t, j):
                if j == 0:
                    pe.wait_ge(h_ok["C"], t + 1)
                    if first(t):
                        pe.wait_ge(ld["c"], 32)
                    else:
                        pe.wait_ge(tmp_ok["C"], t)
                elif j >= 2:
                    pe.wait_ge(g_ok, HJ * t + j - 1)
                for half in range(2):
                    for k in range(KC):
                        m = half * HID + j * P
                        ins = mm(PS["C"][:, j % 2, half * P:(half + 1) * P], w_m1[:, k, m:m + P], HT["C"][:, k, :],
                                 start=(k == 0), stop=(k == KC - 1))
                ins.then_inc(u_ps, 1)

            def down(t):
                pe.wait_ge(g_ok, HJ * t + HJ)
                for j in range(HJ):
                    ins = mm(PS["C"][:, 0, 0:CH], G[:, j, :], w_m2[:, j, :], start=(j == 0), stop=(j == HJ - 1))
                ins.then_inc(y_ps["C"], 1)

            def body(tile):
                def run(step, s, *more):
                    if s in tile:
                        step(s, tile[s], *more)
                for s in "BDCA":
                    run(transpose_h, s)
                run(project_q, "B"); run(project_q, "A"); run(project_q, "D")
                run(scores, "B", 0); run(scores, "A", 0); run(scores, "D", 0)
                run(scores, "B", 1); run(scores, "A", 1); run(scores, "D", 1)
                if "C" in tile:
                    for j in range(HJ):
                        up(tile["C"], j)
                run(transpose_p, "A", 0); run(transpose_p, "D", 0)
                run(transpose_p, "A", 1); run(transpose_p, "D", 1)
                run(weigh_values, "A"); run(weigh_values, "D")
                run(transpose_p, "B", 0)
                if "C" in tile:
                    down(tile["C"])
                run(transpose_o, "A"); run(transpose_o, "D")
                run(transpose_p, "B", 1)
                run(project_o, "A"); run(project_o, "D")
                run(weigh_values, "B")
                run(transpose_o, "B")
                run(project_o, "B")

            setup()
            iterate(pe, body)


def _chunks(w):
    return np.ascontiguousarray(w.reshape(-1, P, w.shape[-1]).transpose(1, 0, 2))


def _laid_out(i):
    n = {k: np.asarray(v) for k, v in i.items()}
    L0 = {k[9:]: v for k, v in n.items() if k.startswith("L0_xcond_")}
    L1 = {k[9:]: v for k, v in n.items() if k.startswith("L1_xcond_")}
    parts = lambda v, k: np.split(v, k, axis=-1)
    ada, bada = parts(L0["w_ada"], 9), parts(L0["b_ada"], 9)
    wq, bq = parts(L1["Wss_q"], 2), parts(L1["bss_q"], 2)
    wk, bk = parts(L1["Wss_kv"], 2), parts(L1["bss_kv"], 2)
    bqkv, bkv0, bkv1, bm1 = parts(L0["b_qkv"], 3), parts(L0["b_kv"], 2), parts(L1["bkv"], 2), parts(L0["b_m1"], 2)
    flat = np.concatenate([bada[1], bada[4], bada[7], bq[0], bk[0], bada[0], bada[3], bada[6], bq[1], bk[1],
                           bqkv[0], bqkv[1], bqkv[2], L0["b_q"], bkv0[0], bkv0[1], L1["bq"], bkv1[0], bkv1[1],
                           bm1[0], bm1[1]])
    pair = np.arange(NCH)[None, :, None] * P + np.arange(P)[:, None, None]
    head = np.array(H0)[None, :, None] + np.arange(NHM)[None, None, :]
    return {
        "x": n["x"],
        "condT": np.ascontiguousarray(n["cond_1024"].T.reshape(KC, P, BATCH).transpose(1, 0, 2)),
        "ctxT": np.ascontiguousarray(n["ctx_1024"].transpose(2, 0, 1).reshape(KC, P, BATCH, LC).transpose(1, 0, 2, 3)),
        "ctxn": np.ascontiguousarray(n["ctx_1024"].transpose(1, 0, 2)),
        "cols": np.ascontiguousarray(flat.reshape(-1, P).T),
        "rows": np.stack([bada[2], bada[5], bada[8], L0["b_so"], L0["b_co"], L0["b_m2"], L1["bp"]])[None],
        "w_mod": _chunks(np.concatenate([ada[1], ada[4], ada[7], wq[0], wk[0], ada[0], ada[3], ada[6], wq[1], wk[1]], 1)),
        "w_gate": _chunks(np.concatenate([ada[2], ada[5], ada[8]], 1)),
        "w_qkv": _chunks(L0["w_qkv"]), "w_so": _chunks(L0["w_so"]), "w_q": _chunks(L0["w_q"]),
        "w_kv": _chunks(L0["w_kv"]), "w_co": _chunks(L0["w_co"]), "w_m1": _chunks(L0["w_m1"]),
        "w_m2": _chunks(L0["w_m2"]), "Wq": _chunks(L1["Wq"]), "Wkv": _chunks(L1["Wkv"]), "Wp": _chunks(L1["Wp"]),
        "ident": np.eye(P, dtype=np.float32),
        "mask4": (np.arange(P)[:, None] % 64 // HD == np.arange(4)[None, :]).astype(np.float32),
        "vmask": ((pair < PAIRS) & (pair // LC == head)).astype(np.float32),
    }


def kernel(**inputs):
    from concourse import bacc
    from concourse.bass_utils import run_bass_kernel_spmd

    nc = bacc.Bacc("TRN2", target_bir_lowering=False, num_devices=1)
    arrays, aps = {}, {}
    for name, arr in _laid_out(inputs).items():
        arrays[f"in_{name}"] = arr
        aps[name] = nc.dram_tensor(f"in_{name}", arr.shape, mybir.dt.from_np(arr.dtype), kind="ExternalInput").ap()
    out = nc.dram_tensor("out_0", (BATCH, LEN, CH), F32, kind="ExternalOutput").ap()
    block_kernel(nc, aps, out)
    r = run_bass_kernel_spmd(nc, [arrays], core_ids=[0])
    return r.results[0]["out_0"]
```

```python
from contextlib import ExitStack

import numpy as np
import concourse.bass as bass
from concourse import mybir

F32 = mybir.dt.float32
ALU = mybir.AluOpType
ACT = mybir.ActivationFunctionType
AX = mybir.AxisListType

BATCH, LEN, CH, HEADS, LC = 4, 1024, 256, 16, 77
P = 128
HD = CH // HEADS
KC = CH // P
HH = HEADS // KC
TPB = LEN // P
TILES = BATCH * TPB
SHIFT, TOPK, HID = 64, 16, 1024
HJ = HID // P
PAIRS = HEADS * LC
NCH = -(-PAIRS // P)
TAIL = PAIRS - (NCH - 1) * P
V1 = HD + 1
H0 = [P * c // LC for c in range(NCH)]
NH = [min(P * c + P - 1, PAIRS - 1) // LC - H0[c] + 1 for c in range(NCH)]
NHM = max(NH)
SCALE = 1.0 / float(HD) ** 0.5
LOW = -3.0e38
EPS0, EPS1 = 1e-6, 1e-5

COLS = [("mod_scale", 10), ("mod_shift", 10), ("bq_a", 2), ("bk_a", 2), ("bv_a", 2), ("bq_b", 2), ("bk_b", 2),
        ("bv_b", 2), ("bq_d", 2), ("bk_d", 2), ("bv_d", 2), ("bm1_a", HJ), ("bm1_b", HJ)]
COL = {}
for _name, _n in COLS:
    COL[_name] = sum(n for k, n in COLS[:len(COL)])
NCOLS = sum(n for _, n in COLS)


def block_kernel(nc, a, out):
    ctx = ExitStack()
    with ctx:
        def sb(name, shape, dt=F32, stack=ctx):
            return stack.enter_context(nc.sbuf_tensor(name, shape, dt))

        def sem(name):
            return ctx.enter_context(nc.semaphore(name))

        ps = ctx.enter_context(nc.psum_tensor("ps", [P, 8, 512], F32))
        PS = {s: ps[:, 2 * n:2 * n + 2, :] for n, s in enumerate("ABCD")}
        scratch = {s: nc.dram_tensor(f"v_flat_{s}", [BATCH, HEADS, LC, HD], F32, kind="Internal").ap() for s in "BD"}

        w_qkv = sb("w_qkv_sb", [P, KC, 3 * CH])
        w_so = sb("w_so_sb", [P, KC, CH])
        w_q = sb("w_q_sb", [P, KC, CH])
        w_co = sb("w_co_sb", [P, KC, CH])
        w_m1 = sb("w_m1_sb", [P, KC, 2 * HID])
        w_m2 = sb("w_m2_sb", [P, HJ, CH])
        w_qd = sb("w_qd_sb", [P, KC, CH])
        w_pd = sb("w_pd_sb", [P, KC, CH])
        cols = sb("cols_sb", [P, NCOLS])
        ident = sb("ident_sb", [P, P])
        mask4 = sb("mask4_sb", [P, 4])
        scaleT = sb("scaleT", [P, 10, BATCH])
        shiftT = sb("shiftT", [P, 10, BATCH])
        gate = sb("gate", [P, 3, BATCH, CH])
        gate_b = sb("gate_b", [P, 3, BATCH, CH])
        bp_row = sb("bp_row", [P, CH])
        kT = {s: sb(f"kT_{s}", [P, KC, BATCH, LC]) for s in "BD"}
        vblk = {s: sb(f"vblk_{s}", [P, BATCH, NCH, NHM * V1]) for s in "BD"}
        half_neg = sb("half_neg", [P, BATCH])

        eps = sb("eps", [P, 2])
        carrier = sb("carrier", [P, 1 + 4 + 4 * KC])

        X, XN, XG, HT, TMP, ST, MV, VE, RS = ({} for _ in range(9))

        def work(s):
            X[s] = sb(f"x_{s}", [P, CH])
            XN[s] = sb(f"xn_{s}", [P, CH])
            XG[s] = sb(f"xg_{s}", [P, CH])
            HT[s] = sb(f"hT_{s}", [P, KC, P])
            TMP[s] = sb(f"tmp_{s}", [P, CH])
            ST[s] = sb(f"st_{s}", [P, 6])
            MV[s] = sb(f"mv_{s}", [P, 2])
            VE[s] = sb(f"ve_{s}", [P, 1])
            RS[s] = sb(f"rstd_{s}", [P, 1])

        QT, KB, PR, PT, O, OT, MX, RC = ({} for _ in range(8))

        def attention_work(s, pairs):
            QT[s] = sb(f"qT_{s}", [P, KC, P])
            KB[s] = sb(f"kblk_{s}", [P, KC, 4, pairs])
            O[s] = sb(f"o_{s}", [P, HEADS, HD])
            OT[s] = sb(f"oT_{s}", [P, KC, P])
            MX[s] = sb(f"mx_{s}", [P, HEADS, 8])
            RC[s] = sb(f"rc_{s}", [P, HEADS, 1])
            if pairs == P:
                PR[s] = sb(f"p_{s}", [P, HEADS, P])
                PT[s] = sb(f"pT_{s}", [P, HEADS, P])
            else:
                PR[s] = sb(f"p_{s}", [P, NCH * P])
                PT[s] = sb(f"pT_{s}", [P, NCH, P])

        work("A")
        attention_work("A", P)
        kTa = sb("kT_A", [P, KC, P])
        va = sb("v_A", [P, HEADS, V1])

        with ExitStack() as early:
            w_mod = sb("w_mod_sb", [P, KC, 10 * CH], F32, early)
            w_gate = sb("w_gate_sb", [P, KC, 3 * CH], F32, early)
            w_kv = {s: sb(f"w_kv_{s}_sb", [P, KC, 2 * CH], F32, early) for s in "BD"}
            rows = sb("rows_sb", [P, 6, CH], F32, early)
            condT = sb("condT_sb", [P, KC, BATCH], F32, early)
            scT = sb("scT", [P, KC, BATCH], F32, early)
            screp = sb("screp", [P, KC, BATCH, P], F32, early)
            ctxT = sb("ctxT_sb", [P, KC, BATCH, LC], F32, early)
            ctxn = sb("ctx_sb", [LC, BATCH, CH], F32, early)
            cn = sb("ctx_norm", [LC, BATCH, CH], F32, early)
            kvT = sb("kvT", [P, KC, BATCH, LC], F32, early)
            cst = sb("ctx_st", [LC, BATCH, 6], F32, early)
            cmv = sb("ctx_mv", [LC, BATCH, 2], F32, early)
            cve = sb("ctx_ve", [LC, BATCH], F32, early)
            crs = sb("ctx_rstd", [LC, BATCH], F32, early)
            vn = {s: sb(f"v_nat_{s}", [LC, BATCH, CH], F32, early) for s in "BD"}
            vf = {s: sb(f"v_flat_sb_{s}", [P, BATCH, NCH, V1], F32, early) for s in "BD"}
            vmask = sb("vmask_sb", [P, NCH, NHM], F32, early)

        work("B")
        attention_work("B", LC)
        S = sb("scores_B", [P, HEADS, LC])
        R = sb("scores_left_B", [P, HEADS, LC])
        MX2 = sb("mx2_B", [P, HEADS, 8])
        work("C")
        SA = sb("silu_C", [P, HJ, P])
        G = sb("hidden_C", [P, HJ, P])
        work("D")
        attention_work("D", LC)
        Y = sb("y_D", [P, CH])

        ld = {n: sem(f"ld_{n}") for n in ("small", "mod", "gate", "qkv", "so", "b", "kv_b", "kv_d", "c", "d", "ctx")}
        silu_done, rep_done = sem("silu_done"), sem("rep_done")
        mod_ps, mod_done, gate_ps, gate_done, gb_done = (sem(n) for n in (
            "mod_ps", "mod_done", "gate_ps", "gate_done", "gb_done"))
        zeroed = sem("zeroed")
        cstat, crstd, cnorm, ct_ps, kv_hT = (sem(n) for n in ("cstat", "crstd", "cnorm", "ct_ps", "kv_hT"))
        ck_ps, ck_done, cv_ps, cv_done, v_out, v_in, vb_done = (
            {s: sem(f"{n}_{s}") for s in "BD"} for n in ("ck_ps", "ck_done", "cv_ps", "cv_done", "v_out", "v_in", "vb_done"))
        pool_self, dve_self = sem("pool_self"), sem("dve_self")

        def per_stage(name, stages="ABCD"):
            return {s: sem(f"{name}_{s}") for s in stages}

        x_in = per_stage("x_in")
        stats = per_stage("stats")
        rstd = per_stage("rstd")
        xn_ok = per_stage("xn_ok")
        xg_ok = per_stage("xg_ok")
        h_ps = per_stage("h_ps")
        h_ok = per_stage("h_ok")
        q_ps = per_stage("q_ps", "ABD")
        q_ok = per_stage("q_ok", "ABD")
        kb_ok = per_stage("kb_ok", "ABD")
        s_ps = per_stage("s_ps", "ABD")
        s_rd = per_stage("s_rd", "ABD")
        mx_ok = per_stage("mx_ok", "AD")
        p_ok = per_stage("p_ok", "ABD")
        pt_ps = per_stage("pt_ps", "ABD")
        pt_ok = per_stage("pt_ok", "ABD")
        pv_ps = per_stage("pv_ps", "ABD")
        rc_ok = per_stage("rc_ok", "ABD")
        o_ok = per_stage("o_ok", "ABD")
        ot_ps = per_stage("ot_ps", "ABD")
        ot_ok = per_stage("ot_ok", "ABD")
        y_ps = per_stage("y_ps")
        tmp_ok = per_stage("tmp_ok")
        top_ok = [sem(f"top_ok_{c}") for c in range(KC)]
        sm_ok = sem("sm_ok")
        e_ok = sem("e_ok")
        u_ps, sa_ok, g_ok = sem("u_ps"), sem("sa_ok"), sem("g_ok")
        y_out = sem("y_out")

        NEXT = {"A": "B", "B": "C", "C": "D"}
        LN = {"A": 0, "B": 1, "C": 2, "D": 3}
        EPS = {"A": EPS0, "B": EPS0, "C": EPS0, "D": EPS1}
        BQ = {"A": "bq_a", "B": "bq_b", "D": "bq_d"}
        BV = {"A": "bv_a", "B": "bv_b", "D": "bv_d"}
        WO = {"A": w_so, "B": w_co, "D": w_pd}

        def col(name, n=0):
            return cols[:, COL[name] + n:COL[name] + n + 1]

        def pick(view, t):
            b = t // TPB
            return view[:, b, :] if isinstance(b, int) else view[:, bass.ds(b, 1), :].rearrange("p b n -> p (b n)")

        def mod_col(table, idx, t):
            return pick(table[:, idx, :].rearrange("p (b n) -> p b n", n=1), t)

        DEPTH = 4

        def iterate(engine, body):
            for i in range(DEPTH + 1):
                body(i)
            with engine.Fori(DEPTH + 1, TILES) as i:
                body(i)
            for i in range(TILES, TILES + DEPTH):
                body(i)

        def run(step, s, i, lag, *more):
            t = i - lag
            if not isinstance(t, int) or 0 <= t < TILES:
                step(s, t, *more)

        def settle(dve, semaphore, value, slot):
            dve.wait_ge(semaphore, value)
            if not isinstance(value, int):
                nc.vector.tensor_copy(carrier[:, 1 + slot:2 + slot], carrier[:, 0:1])

        def first(t):
            return isinstance(t, int) and t == 0

        def pairs_view(ap, c):
            return ap[:, c * HH * LC:(c + 1) * HH * LC].rearrange("p (h k) -> p h k", h=HH)

        def score_banks(s, c=None):
            return PS[s][:, :, 0:4 * LC]

        block = ctx.enter_context(nc.Block())

        @block.sync
        def _(sp):
            def load_weights(dst, src, s):
                sp.dma_start(dst, src).then_inc(ld[s], 16)

            x_blocks = a["x"].rearrange("b (u p) c -> (b u) p c", p=SHIFT)
            out_blocks = out.rearrange("b (u p) c -> (b u) p c", p=SHIFT)
            PER = LEN // SHIFT

            def halves(t):
                second = (t // TPB) * PER + (2 * t + 2) % PER
                return 2 * t + 1, second

            def block_of(view, u):
                return view[u] if isinstance(u, int) else view[bass.ds(u, 1)].rearrange("a p c -> (a p) c")

            def load_x(t):
                if not first(t):
                    sp.wait_ge(xn_ok["A"], t)
                    sp.wait_ge(xg_ok["A"], t)
                for n, u in enumerate(halves(t)):
                    sp.dma_start(X["A"][n * SHIFT:(n + 1) * SHIFT, :], block_of(x_blocks, u)).then_inc(x_in["A"], 16)

            def store_y(t):
                sp.wait_ge(tmp_ok["D"], t + 1)
                for n, u in enumerate(halves(t)):
                    sp.dma_start(block_of(out_blocks, u), Y[n * SHIFT:(n + 1) * SHIFT, :]).then_inc(y_out, 16)

            load_weights(condT[:], a["condT"], "small")
            load_weights(cols[:], a["cols"], "small")
            load_weights(rows[:], a["rows"][:, 0:6, :].partition_broadcast(P).rearrange("p a n c -> p (a n) c"), "small")
            load_weights(ident[:], a["ident"], "small")
            load_weights(mask4[:], a["mask4"], "small")
            load_weights(w_mod[:, 0, :], a["w_mod"][:, 0, :], "mod")
            load_weights(w_mod[:, 1, :], a["w_mod"][:, 1, :], "mod")
            load_weights(w_qkv[:], a["w_qkv"], "qkv")
            load_weights(w_gate[:], a["w_gate"], "gate")
            load_weights(w_so[:], a["w_so"], "so")
            load_weights(w_kv["B"][:], a["w_kv"], "kv_b")
            load_weights(w_kv["D"][:], a["Wkv"], "kv_d")
            load_weights(w_q[:], a["w_q"], "b")
            load_weights(w_co[:], a["w_co"], "b")
            load_weights(w_m1[:], a["w_m1"], "c")
            load_weights(w_m2[:], a["w_m2"], "c")
            load_weights(w_qd[:], a["Wq"], "d")
            load_weights(w_pd[:], a["Wp"], "d")

            def load(s, t):
                load_x(t)

            def store(s, t):
                store_y(t)

            def body(i):
                run(load, "A", i, 0)
                run(store, "D", i, 4)

            iterate(sp, body)
            sp.wait_ge(y_out, 32 * TILES)

        @block.gpsimd
        def _(pool):
            g = nc.gpsimd
            selfs = [0]

            def link(ins):
                selfs[0] += 1
                ins.then_inc(pool_self, 1)
                pool.wait_ge(pool_self, selfs[0])

            g.dma_start(ctxn[:], a["ctxn"]).then_inc(ld["ctx"], 16)
            g.dma_start(ctxT[:], a["ctxT"]).then_inc(ld["ctx"], 16)
            g.dma_start(vmask[:], a["vmask"]).then_inc(ld["ctx"], 16)
            g.dma_start(bp_row[:], a["rows"][:, 6, :].partition_broadcast(P).rearrange("p a c -> p (a c)")).then_inc(ld["ctx"], 16)
            g.memset(half_neg[:], -0.5).then_inc(zeroed, 1)
            g.memset(va[:, :, HD:V1], 1.0).then_inc(zeroed, 1)
            for s in "BD":
                link(g.memset(vf[s][:], 0.0))
                g.memset(vf[s][:, :, :, HD:V1], 1.0).then_inc(zeroed, 1)
            g.memset(carrier[:], 0.0).then_inc(zeroed, 1)
            g.memset(eps[:, 0:1], EPS0).then_inc(zeroed, 1)
            g.memset(eps[:, 1:2], EPS1).then_inc(zeroed, 1)
            pool.wait_ge(zeroed, 7)

            def setup_gates():
                pool.wait_ge(gate_done, 1)
                pool.wait_ge(ld["small"], 16 * 5)
                for n in range(3):
                    ins = g.tensor_tensor(gate_b[:, n], gate[:, n], rows[:, 3 + n:4 + n, :].to_broadcast([P, BATCH, CH]), ALU.mult)
                ins.then_inc(gb_done, 1)
                pool.wait_ge(gb_done, 1)

            def setup_context_rstd():
                pool.wait_ge(cstat, 2 * BATCH)
                link(g.tensor_scalar(cve[:], cmv[:, :, 1], EPS1, None, ALU.add))
                g.tensor_tensor(crs[:], cve[:], half_neg[0:LC, :], ALU.pow).then_inc(crstd, 1)

            def setup_flat(s):
                pool.wait_ge(cv_done[s], 1)
                for b in range(BATCH):
                    g.dma_start(scratch[s][b].rearrange("h k d -> k h d"),
                                vn[s][:, b, :].rearrange("k (h d) -> k h d", h=HEADS)).then_inc(v_out[s], 16)
                pool.wait_ge(v_out[s], 16 * BATCH)
                full = (NCH - 1) * P
                for b in range(BATCH):
                    flat = scratch[s][b].rearrange("h k d -> (h k) d")
                    g.dma_start(vf[s][:, b, 0:NCH - 1, 0:HD],
                                flat[0:full].rearrange("(c p) d -> p c d", p=P)).then_inc(v_in[s], 16)
                    g.dma_start(vf[s][0:TAIL, b, NCH - 1, 0:HD], flat[full:PAIRS]).then_inc(v_in[s], 16)

            def setup_blocks(s):
                pool.wait_ge(v_in[s], 32 * BATCH)
                pool.wait_ge(ld["ctx"], 16 * 4)
                for b in range(BATCH):
                    ins = g.tensor_tensor(vblk[s][:, b].rearrange("p c (n v) -> p c n v", n=NHM),
                                          vf[s][:, b].unsqueeze(2).to_broadcast([P, NCH, NHM, V1]),
                                          vmask[:].unsqueeze(3).to_broadcast([P, NCH, NHM, V1]), ALU.mult)
                ins.then_inc(vb_done[s], 1)

            def reciprocal_root(s, t):
                pool.wait_ge(stats[s], 2 * t + 2)
                g.tensor_tensor(VE[s][:], MV[s][:, 1:2], eps[:, LN[s] // 3:LN[s] // 3 + 1], ALU.add).then_inc(rstd[s], 1)
                pool.wait_ge(rstd[s], 2 * t + 1)
                g.tensor_tensor(RS[s][:], VE[s][:], half_neg[:, 0:1], ALU.pow).then_inc(rstd[s], 1)

            def gated_bias(s, t):
                if s == "A":
                    pool.wait_ge(x_in[s], 32 * t + 32)
                if s != "D" and not first(t):
                    pool.wait_ge(x_in[NEXT[s]], t)
                if s == "D":
                    if not first(t):
                        pool.wait_ge(tmp_ok["D"], t)
                    bias = bp_row[:]
                    pool.wait_ge(x_in[s], t + 1)
                else:
                    bias = pick(gate_b[:, LN[s]], t)
                    if s != "A":
                        pool.wait_ge(x_in[s], t + 1)
                g.tensor_tensor(XG[s][:], X[s][:], bias, ALU.add).then_inc(xg_ok[s], 1)

            def key_blocks(s, t):
                if s == "A":
                    pool.wait_ge(q_ok[s], t + 1)
                else:
                    pool.wait_ge(ck_done[s], 1)
                    if not first(t):
                        pool.wait_ge(s_ps[s], 2 * t)
                for c in range(KC):
                    if s == "A":
                        keys = kTa[:, c, :]
                        n = P
                    else:
                        keys = pick(kT[s][:, c], t)
                        n = LC
                    ins = g.tensor_tensor(KB[s][:, c], keys.unsqueeze(1).to_broadcast([P, 4, n]),
                                          mask4[:].unsqueeze(2).to_broadcast([P, 4, n]), ALU.mult)
                ins.then_inc(kb_ok[s], 1)

            def less_max(s, t, c):
                pool.wait_ge(top_ok[c], 4 * t + 1)
                g.tensor_tensor(pairs_view(PR["B"], c), S[:, c * HH:(c + 1) * HH, :],
                                MX["B"][:, c * HH:(c + 1) * HH, 0:1].to_broadcast([P, HH, LC]),
                                ALU.subtract).then_inc(sm_ok, 1)

            def residual(s, t):
                pool.wait_ge(tmp_ok[s], t + 1)
                nxt = NEXT[s]
                pool.wait_ge(xg_ok[s], t + 1)
                if not first(t):
                    pool.wait_ge(xn_ok[nxt], t)
                    pool.wait_ge(xg_ok[nxt], t)
                g.tensor_tensor(X[nxt][:], XG[s][:], TMP[s][:], ALU.add).then_inc(x_in[nxt], 1)

            def body(i):
                run(gated_bias, "B", i, 3)
                run(residual, "C", i, 4)
                run(reciprocal_root, "D", i, 4)
                run(residual, "B", i, 3)
                run(reciprocal_root, "A", i, 1)
                run(reciprocal_root, "C", i, 3)
                run(key_blocks, "B", i, 2)
                run(residual, "A", i, 2)
                run(reciprocal_root, "B", i, 2)
                run(less_max, "B", i, 2, 0)
                run(gated_bias, "D", i, 4)
                run(gated_bias, "A", i, 1)
                run(less_max, "B", i, 2, 1)
                run(gated_bias, "C", i, 3)
                run(key_blocks, "D", i, 3)
                run(key_blocks, "A", i, 1)

            setup_gates()
            setup_context_rstd()
            setup_flat("B")
            setup_blocks("B")
            setup_flat("D")
            setup_blocks("D")
            g.memset(PR["B"][:, PAIRS:NCH * P], 0.0).then_inc(zeroed, 1)
            g.memset(PR["D"][:, PAIRS:NCH * P], 0.0).then_inc(zeroed, 1)
            iterate(pool, body)

        @block.scalar
        def _(act):
            sc = nc.scalar

            def setup():
                act.wait_ge(ld["small"], 16 * 5)
                sc.activation(scT[:], condT[:], ACT.Silu).then_inc(silu_done, 1)
                act.wait_ge(ck_ps["B"], 1)
                for c in range(KC):
                    ins = sc.activation(kT["B"][:, c].rearrange("p b k -> p (b k)"), PS["A"][:, c, 0:BATCH * LC],
                                        ACT.Identity, bias=col("bk_b", c))
                ins.then_inc(ck_done["B"], 1)
                act.wait_ge(cv_ps["B"], 1)
                sc.copy(vn["B"][:].rearrange("k (m n) c -> k m (n c)", m=2), PS["B"][0:LC]).then_inc(cv_done["B"], 1)
                act.wait_ge(ct_ps, 1)
                act.wait_ge(mod_done, 1)
                for c in range(KC):
                    for b in range(BATCH):
                        ins = sc.activation(kvT[:, c, b, :], PS["C"][:, c, b * LC:(b + 1) * LC], ACT.Identity,
                                            scale=scaleT[:, 8 + c, b:b + 1], bias=shiftT[:, 8 + c, b:b + 1])
                ins.then_inc(kv_hT, 1)
                act.wait_ge(ck_ps["D"], 1)
                for c in range(KC):
                    ins = sc.activation(kT["D"][:, c].rearrange("p b k -> p (b k)"), PS["A"][:, c, 0:BATCH * LC],
                                        ACT.Identity, bias=col("bk_d", c))
                ins.then_inc(ck_done["D"], 1)
                act.wait_ge(cv_ps["D"], 1)
                sc.copy(vn["D"][:].rearrange("k (m n) c -> k m (n c)", m=2), PS["D"][0:LC]).then_inc(cv_done["D"], 1)

            def modulate(s, t):
                act.wait_ge(h_ps[s], t + 1)
                for c in range(KC):
                    ins = sc.activation(HT[s][:, c, :], PS[s][:, 1, c * P:(c + 1) * P], ACT.Identity,
                                        scale=mod_col(scaleT, 2 * LN[s] + c, t), bias=mod_col(shiftT, 2 * LN[s] + c, t))
                ins.then_inc(h_ok[s], 1)

            def queries(s, t):
                act.wait_ge(q_ps[s], t + 1)
                for c in range(KC):
                    ins = sc.activation(QT[s][:, c, :], PS[s][:, 0, c * P:(c + 1) * P], ACT.Identity, bias=col(BQ[s], c))
                if s == "A":
                    for c in range(KC):
                        sc.activation(kTa[:, c, :], PS[s][:, 0, (KC + c) * P:(KC + c + 1) * P], ACT.Identity,
                                      bias=col("bk_a", c))
                    ins = sc.copy(va[:, :, 0:HD], PS[s][:, 1, CH:2 * CH].rearrange("p (h d) -> p h d", h=HEADS))
                ins.then_inc(q_ok[s], 1)

            def exponentials(s, t, c):
                if s == "A":
                    act.wait_ge(s_rd[s], 2 * t + c + 1)
                    w = PR[s][:, c * HH:(c + 1) * HH, :]
                    sc.activation(w, w, ACT.Exp, scale=SCALE).then_inc(p_ok[s], 1)
                elif s == "B":
                    act.wait_ge(sm_ok, 2 * t + c + 1)
                    w = pairs_view(PR[s], c)
                    sc.activation(w, w, ACT.Exp, scale=SCALE).then_inc(e_ok, 1)
                else:
                    act.wait_ge(s_rd[s], 2 * t + c + 1)
                    w = pairs_view(PR[s], c)
                    sc.activation(w, w, ACT.Exp, scale=SCALE).then_inc(p_ok[s], 1)

            def copy_scores(s, t, c):
                act.wait_ge(s_ps["B"], 2 * t + c + 1)
                sc.copy(S[:, c * HH:(c + 1) * HH, :].rearrange("p (j h) k -> p j (h k)", j=2),
                        score_banks("B")).then_inc(s_rd["B"], 1)

            def weights_out(s, t, c):
                act.wait_ge(pt_ps[s], 2 * t + c + 1)
                if s == "A":
                    ins = sc.copy(PT[s][:, c * HH:(c + 1) * HH, :].rearrange("p (j h) q -> p j (h q)", j=2), PS[s])
                elif c == 0:
                    ins = sc.copy(PT[s][:, 0:4, :].rearrange("p c q -> p (c q)"), PS[s][:, 0, :])
                else:
                    sc.copy(PT[s][:, 4:8, :].rearrange("p c q -> p (c q)"), PS[s][:, 1, :])
                    ins = sc.copy(PT[s][:, 8:NCH, :].rearrange("p c q -> p (c q)"), PS[s][:, 0, 0:(NCH - 8) * P])
                ins.then_inc(pt_ok[s], 1)

            def output_t(s, t):
                act.wait_ge(ot_ps[s], t + 1)
                for c in range(KC):
                    ins = sc.activation(OT[s][:, c, :], PS[s][:, 1, c * P:(c + 1) * P], ACT.Identity, bias=col(BV[s], c))
                ins.then_inc(ot_ok[s], 1)

            def silu(s, t, j):
                act.wait_ge(u_ps, HJ * t + j + 1)
                sc.activation(SA[:, j, :], PS["C"][:, j % 2, 0:P], ACT.Silu, bias=col("bm1_a", j)).then_inc(sa_ok, 1)

            def body(i):
                run(weights_out, "D", i, 3, 0)
                run(silu, "C", i, 2, 0)
                run(silu, "C", i, 2, 1)
                run(modulate, "B", i, 1)
                run(weights_out, "D", i, 3, 1)
                run(silu, "C", i, 2, 2)
                run(queries, "B", i, 1)
                run(silu, "C", i, 2, 3)
                run(copy_scores, "B", i, 1, 0)
                run(silu, "C", i, 2, 4)
                run(silu, "C", i, 2, 5)
                run(copy_scores, "B", i, 1, 1)
                run(modulate, "A", i, 0)
                run(silu, "C", i, 2, 6)
                run(silu, "C", i, 2, 7)
                run(exponentials, "B", i, 1, 0)
                run(queries, "A", i, 0)
                run(exponentials, "B", i, 1, 1)
                run(weights_out, "B", i, 1, 0)
                run(output_t, "D", i, 3)
                run(weights_out, "B", i, 1, 1)
                run(exponentials, "A", i, 0, 0)
                run(modulate, "D", i, 2)
                run(exponentials, "A", i, 0, 1)
                run(weights_out, "A", i, 0, 0)
                run(queries, "D", i, 2)
                run(output_t, "B", i, 1)
                run(weights_out, "A", i, 0, 1)
                run(output_t, "A", i, 0)
                run(exponentials, "D", i, 2, 0)
                run(modulate, "C", i, 1)
                run(exponentials, "D", i, 2, 1)

            setup()
            iterate(act, body)

        @block.vector
        def _(dve):
            v = nc.vector

            def setup():
                dve.wait_ge(silu_done, 1)
                for c in range(KC):
                    ins = v.tensor_copy(screp[:, c], scT[:, c, :].unsqueeze(2).to_broadcast([P, BATCH, P]))
                ins.then_inc(rep_done, 1)
                dve.wait_ge(ld["ctx"], 16 * 4)
                for b in range(BATCH):
                    ins = v.bn_stats(cst[:, b, :], ctxn[:, b, :]).then_inc(cstat, 1)
                dve.wait_ge(cstat, BATCH)
                for b in range(BATCH):
                    v.bn_aggr(cmv[:, b, :], cst[:, b, :]).then_inc(cstat, 1)
                dve.wait_ge(mod_ps, 1)
                dve.wait_ge(ld["small"], 16 * 5)
                mod = PS["A"][:, 0, 0:80].rearrange("p (m i b) -> p m i b", m=2, b=BATCH)
                v.scalar_tensor_tensor(out=scaleT[:], in0=mod[:, 0], scalar=1.0,
                                       in1=cols[:, COL["mod_scale"]:COL["mod_scale"] + 10].unsqueeze(2).to_broadcast(
                                           [P, 10, BATCH]), op0=ALU.add, op1=ALU.add)
                v.tensor_tensor(shiftT[:], mod[:, 1], cols[:, COL["mod_shift"]:COL["mod_shift"] + 10].unsqueeze(2)
                                .to_broadcast([P, 10, BATCH]), ALU.add).then_inc(mod_done, 1)
                dve.wait_ge(gate_ps, 1)
                for n in range(3):
                    ins = v.tensor_tensor(gate[:, n].rearrange("p (m b) c -> p m b c", m=2),
                                          ps[:, 2 + 2 * n:4 + 2 * n, :].rearrange("p m (b c) -> p m b c", b=2),
                                          rows[:, n:n + 1, :].unsqueeze(1).to_broadcast([P, 2, 2, CH]), ALU.add)
                ins.then_inc(gate_done, 1)
                dve.wait_ge(crstd, 1)
                for b in range(BATCH):
                    ins = v.tensor_scalar(cn[:, b, :], ctxn[:, b, :], cmv[:, b, 0:1], crs[:, b:b + 1],
                                          ALU.subtract, ALU.mult)
                ins.then_inc(cnorm, 1)

            def statistics(s, t):
                dve.wait_ge(x_in[s], 32 * t + 32 if s == "A" else t + 1)
                v.bn_stats(ST[s][:], X[s][:]).then_inc(stats[s], 1)
                if not first(t):
                    dve.wait_ge(xn_ok[s], t)
                settle(dve, stats[s], 2 * t + 1, LN[s])
                v.bn_aggr(MV[s][:], ST[s][:]).then_inc(stats[s], 1)

            def normalise(s, t):
                dve.wait_ge(rstd[s], 2 * t + 2)
                if not first(t):
                    dve.wait_ge(h_ps[s], t)
                v.tensor_scalar(XN[s][:], X[s][:], MV[s][:, 0:1], RS[s][:], ALU.subtract, ALU.mult).then_inc(xn_ok[s], 1)

            def maxima(s, t, c):
                dve.wait_ge(s_ps[s], 2 * t + c + 1)
                view = (PS[s].rearrange("p j (h k) -> p j h k", h=4) if s == "A"
                        else score_banks(s).rearrange("p j (h k) -> p j h k", h=4))
                v.tensor_reduce(MX[s][:, c * HH:(c + 1) * HH, 0].rearrange("p (j h) -> p j h", j=2), view,
                                AX.X, ALU.max).then_inc(mx_ok[s], 1)
                dve.wait_ge(mx_ok[s], 2 * t + c + 1)
                w = PR[s][:, c * HH:(c + 1) * HH, :] if s == "A" else pairs_view(PR[s], c)
                n = P if s == "A" else LC
                v.tensor_tensor(w.rearrange("p (j h) k -> p j h k", j=2), view,
                                MX[s][:, c * HH:(c + 1) * HH, 0:1].rearrange("p (j h) o -> p j h o", j=2)
                                .to_broadcast([P, 2, 4, n]), ALU.subtract).then_inc(s_rd[s], 1)

            def select(s, t, c, step):
                if step == 0:
                    settle(dve, s_rd["B"], 2 * t + c + 1, 4 + 4 * c)
                else:
                    settle(dve, top_ok[c], 4 * t + step, 4 + 4 * c + step)
                for h in range(c * HH, (c + 1) * HH):
                    if step == 0:
                        ins = v.max(MX["B"][:, h, :], S[:, h, :])
                    elif step == 1:
                        ins = v.match_replace(R[:, h, :], MX["B"][:, h, :], S[:, h, :], LOW)
                    elif step == 2:
                        ins = v.max(MX2[:, h, :], R[:, h, :])
                    else:
                        ins = v.match_replace(R[:, h, :], MX2[:, h, :], R[:, h, :], LOW)
                ins.then_inc(top_ok[c], 1)

            def keep_chosen(s, t, c):
                dve.wait_ge(top_ok[c], 4 * t + 4)
                dve.wait_ge(e_ok, 2 * t + c + 1)
                w = PR["B"][:, c * HH * LC:(c + 1) * HH * LC]
                v.scalar_tensor_tensor(out=w, in0=R[:, c * HH:(c + 1) * HH, :].rearrange("p h k -> p (h k)"), scalar=LOW,
                                       in1=w, op0=ALU.is_equal, op1=ALU.mult).then_inc(p_ok["B"], 1)

            def normalise_output(s, t):
                dve.wait_ge(pv_ps[s], t + 1)
                acc = PS[s][:, 0, 0:HEADS * V1].rearrange("p (h v) -> p h v", h=HEADS)
                v.reciprocal(RC[s][:], acc[:, :, HD:V1]).then_inc(rc_ok[s], 1)
                dve.wait_ge(rc_ok[s], t + 1)
                v.tensor_tensor(O[s][:], acc[:, :, 0:HD], RC[s][:].to_broadcast([P, HEADS, HD]),
                                ALU.mult).then_inc(o_ok[s], 1)

            def gated(s, t):
                dve.wait_ge(y_ps[s], t + 1)
                y = PS[s][:, 0, 0:CH]
                if s == "D":
                    dve.wait_ge(xg_ok[s], t + 1)
                    if not first(t):
                        dve.wait_ge(y_out, 32 * t)
                    v.tensor_tensor(Y[:], y, XG[s][:], ALU.add).then_inc(tmp_ok[s], 1)
                    return
                if first(t):
                    dve.wait_ge(gate_done, 1)
                else:
                    dve.wait_ge(x_in[NEXT[s]], t)
                v.tensor_tensor(TMP[s][:], y, pick(gate[:, LN[s]], t), ALU.mult).then_inc(tmp_ok[s], 1)

            def hidden(s, t, j):
                dve.wait_ge(sa_ok, HJ * t + j + 1)
                v.scalar_tensor_tensor(out=G[:, j, :], in0=PS["C"][:, j % 2, P:2 * P], scalar=col("bm1_b", j),
                                       in1=SA[:, j, :], op0=ALU.add, op1=ALU.mult).then_inc(g_ok, 1)

            def body(i):
                run(statistics, "A", i, 0)
                run(gated, "D", i, 4)
                run(normalise_output, "B", i, 2)
                run(maxima, "D", i, 3, 0)
                run(gated, "B", i, 2)
                run(statistics, "C", i, 2)
                run(normalise_output, "A", i, 1)
                run(normalise, "C", i, 2)
                run(maxima, "D", i, 3, 1)
                run(normalise, "A", i, 0)
                run(gated, "A", i, 1)
                run(statistics, "B", i, 1)
                run(normalise, "B", i, 1)
                run(hidden, "C", i, 2, 0)
                run(hidden, "C", i, 2, 1)
                run(hidden, "C", i, 2, 2)
                run(hidden, "C", i, 2, 3)
                run(select, "B", i, 1, 0, 0)
                run(hidden, "C", i, 2, 4)
                run(select, "B", i, 1, 0, 1)
                run(hidden, "C", i, 2, 5)
                run(select, "B", i, 1, 1, 0)
                run(hidden, "C", i, 2, 6)
                run(select, "B", i, 1, 1, 1)
                run(select, "B", i, 1, 0, 2)
                run(hidden, "C", i, 2, 7)
                run(select, "B", i, 1, 1, 2)
                run(select, "B", i, 1, 0, 3)
                run(select, "B", i, 1, 1, 3)
                run(keep_chosen, "B", i, 1, 0)
                run(gated, "C", i, 2)
                run(normalise_output, "D", i, 3)
                run(keep_chosen, "B", i, 1, 1)
                run(maxima, "A", i, 0, 0)
                run(statistics, "D", i, 2)
                run(normalise, "D", i, 2)
                run(maxima, "A", i, 0, 1)

            setup()
            dve.wait_ge(zeroed, 7)
            iterate(dve, body)

        @block.tensor
        def _(pe):
            mm = nc.tensor.matmul

            def setup():
                pe.wait_ge(rep_done, 1)
                pe.wait_ge(ld["mod"], 32)
                for i in range(20):
                    for c in range(KC):
                        ins = mm(PS["A"][:, 0, i * BATCH:(i + 1) * BATCH], w_mod[:, c, i * P:(i + 1) * P], scT[:, c, :],
                                 start=(c == 0), stop=(c == KC - 1))
                ins.then_inc(mod_ps, 1)
                pe.wait_ge(ld["gate"], 16)
                for n in range(3):
                    for b in range(BATCH):
                        for c in range(KC):
                            ins = mm(ps[:, 2 + 2 * n + b // 2, (b % 2) * CH:(b % 2 + 1) * CH], screp[:, c, b, :],
                                     w_gate[:, c, n * CH:(n + 1) * CH], start=(c == 0), stop=(c == KC - 1))
                ins.then_inc(gate_ps, 1)
                pe.wait_ge(mod_done, 1)
                pe.wait_ge(ld["ctx"], 16 * 4)
                pe.wait_ge(ld["kv_b"], 16)
                context(ctxT, "B")
                pe.wait_ge(gate_done, 1)
                context_values(ctxT, "B")
                pe.wait_ge(cnorm, 1)
                pe.wait_ge(ld["small"], 16 * 5)
                for c in range(KC):
                    for b in range(BATCH):
                        ins = nc.tensor.transpose(PS["C"][:, c, b * LC:(b + 1) * LC], cn[:, b, c * P:(c + 1) * P],
                                                  ident[0:LC, 0:LC])
                ins.then_inc(ct_ps, 1)
                pe.wait_ge(kv_hT, 1)
                pe.wait_ge(ld["kv_d"], 16)
                pe.wait_ge(ck_done["B"], 1)
                context(kvT, "D")
                context_values(kvT, "D")
                pe.wait_ge(ck_done["D"], 1)
                pe.wait_ge(cv_done["B"], 1)
                pe.wait_ge(cv_done["D"], 1)

            def context(src, s):
                for c in range(KC):
                    for k in range(KC):
                        ins = mm(PS["A"][:, c, 0:BATCH * LC], w_kv[s][:, k, c * P:(c + 1) * P],
                                 src[:, k].rearrange("p b k -> p (b k)"), start=(k == 0), stop=(k == KC - 1))
                ins.then_inc(ck_ps[s], 1)

            def context_values(src, s):
                for b in range(BATCH):
                    for k in range(KC):
                        ins = mm(PS[s][0:LC, b // 2, (b % 2) * CH:(b % 2 + 1) * CH], src[:, k, b, :],
                                 w_kv[s][:, k, CH:2 * CH], start=(k == 0), stop=(k == KC - 1))
                ins.then_inc(cv_ps[s], 1)

            def transpose_h(s, t):
                pe.wait_ge(xn_ok[s], t + 1)
                for c in range(KC):
                    ins = nc.tensor.transpose(PS[s][:, 1, c * P:(c + 1) * P], XN[s][:, c * P:(c + 1) * P], ident[:])
                ins.then_inc(h_ps[s], 1)

            def project_q(s, t):
                pe.wait_ge(h_ok[s], t + 1)
                if first(t):
                    pe.wait_ge(ld[{"A": "qkv", "B": "b", "D": "d"}[s]], 32 if s != "A" else 16)
                else:
                    pe.wait_ge(tmp_ok[s], t)
                w = {"A": w_qkv, "B": w_q, "D": w_qd}[s]
                for c in range(4 if s == "A" else 2):
                    for k in range(KC):
                        ins = mm(PS[s][:, 0, c * P:(c + 1) * P], w[:, k, c * P:(c + 1) * P], HT[s][:, k, :],
                                 start=(k == 0), stop=(k == KC - 1))
                if s == "A":
                    for k in range(KC):
                        ins = mm(PS[s][:, 1, CH:2 * CH], HT[s][:, k, :], w[:, k, 2 * CH:3 * CH],
                                 start=(k == 0), stop=(k == KC - 1))
                ins.then_inc(q_ps[s], 1)

            def scores(s, t, c):
                if c == 0:
                    pe.wait_ge(q_ok[s], t + 1)
                    pe.wait_ge(kb_ok[s], t + 1)
                else:
                    pe.wait_ge(s_rd[s], 2 * t + 1)
                n = 4 * (P if s == "A" else LC)
                for j in range(2):
                    rows_ = slice(64 * j, 64 * j + 64)
                    ins = mm(PS[s][:, j, 0:n], QT[s][rows_, c, :], KB[s][rows_, c].rearrange("p h k -> p (h k)"),
                             start=True, stop=True)
                ins.then_inc(s_ps[s], 1)

            def transpose_p(s, t, c):
                if c == 0:
                    pe.wait_ge(s_rd[s], 2 * t + 2)
                    if s != "A" and first(t):
                        pe.wait_ge(zeroed, 9)
                else:
                    pe.wait_ge(pt_ok[s], 2 * t + 1)
                pe.wait_ge(p_ok[s], 2 * t + c + 1)
                if s == "A":
                    for h in range(HH):
                        ins = nc.tensor.transpose(PS[s][:, h // 4, (h % 4) * P:(h % 4 + 1) * P],
                                                  PR[s][:, c * HH + h, :], ident[:])
                else:
                    for n in (range(4) if c == 0 else range(4, NCH)):
                        bank = 1 if 4 <= n < 8 else 0
                        ins = nc.tensor.transpose(PS[s][:, bank, (n % 4) * P:(n % 4 + 1) * P],
                                                  PR[s][:, n * P:(n + 1) * P], ident[:])
                ins.then_inc(pt_ps[s], 1)

            def weigh_values(s, t, part, parts):
                if part == 0:
                    pe.wait_ge(pt_ok[s], 2 * t + 2)
                if s == "A":
                    for h in range(part * HEADS // parts, (part + 1) * HEADS // parts):
                        ins = mm(PS[s][:, 0, h * V1:(h + 1) * V1], PT[s][:, h, :], va[:, h, :], start=True, stop=True)
                else:
                    if first(t) and part == 0:
                        pe.wait_ge(vb_done[s], 1)
                    for n in range(part * NCH // parts, (part + 1) * NCH // parts):
                        ins = mm(PS[s][:, 0, H0[n] * V1:(H0[n] + NH[n]) * V1], PT[s][:, n, :],
                                 pick(vblk[s][:, :, n, 0:NH[n] * V1], t), start=(n == 0), stop=(n == NCH - 1),
                                 skip_group_check=True)
                if part == parts - 1:
                    ins.then_inc(pv_ps[s], 1)

            def transpose_o(s, t):
                pe.wait_ge(o_ok[s], t + 1)
                for c in range(KC):
                    ins = nc.tensor.transpose(PS[s][:, 1, c * P:(c + 1) * P],
                                              O[s][:].rearrange("p h d -> p (h d)")[:, c * P:(c + 1) * P], ident[:])
                ins.then_inc(ot_ps[s], 1)

            def project_o(s, t):
                pe.wait_ge(ot_ok[s], t + 1)
                if first(t) and s == "A":
                    pe.wait_ge(ld["so"], 16)
                for k in range(KC):
                    ins = mm(PS[s][:, 0, 0:CH], OT[s][:, k, :], WO[s][:, k, :], start=(k == 0), stop=(k == KC - 1))
                ins.then_inc(y_ps[s], 1)

            def up(s, t, j):
                if j == 0:
                    pe.wait_ge(h_ok["C"], t + 1)
                    if first(t):
                        pe.wait_ge(ld["c"], 32)
                    else:
                        pe.wait_ge(tmp_ok["C"], t)
                elif j >= 2:
                    pe.wait_ge(g_ok, HJ * t + j - 1)
                for half in range(2):
                    for k in range(KC):
                        m = half * HID + j * P
                        ins = mm(PS["C"][:, j % 2, half * P:(half + 1) * P], w_m1[:, k, m:m + P], HT["C"][:, k, :],
                                 start=(k == 0), stop=(k == KC - 1))
                ins.then_inc(u_ps, 1)

            def down(s, t, half):
                if half == 0:
                    pe.wait_ge(g_ok, HJ * t + HJ)
                for j in range(half * HJ // 2, (half + 1) * HJ // 2):
                    ins = mm(PS["C"][:, 0, 0:CH], G[:, j, :], w_m2[:, j, :], start=(j == 0), stop=(j == HJ - 1))
                if half == 1:
                    ins.then_inc(y_ps["C"], 1)

            def body(i):
                run(transpose_h, "A", i, 0)
                run(up, "C", i, 2, 4)
                run(up, "C", i, 2, 5)
                run(scores, "B", i, 1, 1)
                run(weigh_values, "D", i, 3, 0, 2)
                run(up, "C", i, 2, 6)
                run(up, "C", i, 2, 7)
                run(project_q, "A", i, 0)
                run(weigh_values, "D", i, 3, 1, 2)
                run(down, "C", i, 2, 0)
                run(down, "C", i, 2, 1)
                run(scores, "A", i, 0, 0)
                run(transpose_p, "B", i, 1, 0)
                run(transpose_o, "D", i, 3)
                run(transpose_p, "B", i, 1, 1)
                run(project_o, "D", i, 3)
                run(scores, "A", i, 0, 1)
                run(transpose_h, "D", i, 2)
                run(weigh_values, "B", i, 1, 0, 2)
                run(weigh_values, "B", i, 1, 1, 2)
                run(transpose_p, "A", i, 0, 0)
                run(project_q, "D", i, 2)
                run(transpose_o, "B", i, 1)
                run(transpose_p, "A", i, 0, 1)
                run(scores, "D", i, 2, 0)
                run(project_o, "B", i, 1)
                run(weigh_values, "A", i, 0, 0, 4)
                run(weigh_values, "A", i, 0, 1, 4)
                run(weigh_values, "A", i, 0, 2, 4)
                run(weigh_values, "A", i, 0, 3, 4)
                run(scores, "D", i, 2, 1)
                run(transpose_o, "A", i, 0)
                run(transpose_h, "C", i, 1)
                run(project_o, "A", i, 0)
                run(transpose_p, "D", i, 2, 0)
                run(up, "C", i, 1, 0)
                run(up, "C", i, 1, 1)
                run(transpose_p, "D", i, 2, 1)
                run(transpose_h, "B", i, 0)
                run(up, "C", i, 1, 2)
                run(project_q, "B", i, 0)
                run(up, "C", i, 1, 3)
                run(scores, "B", i, 0, 0)

            setup()
            iterate(pe, body)


def _chunks(w):
    return np.ascontiguousarray(w.reshape(-1, P, w.shape[-1]).transpose(1, 0, 2))


def _laid_out(i):
    n = {k: np.asarray(v) for k, v in i.items()}
    L0 = {k[9:]: v for k, v in n.items() if k.startswith("L0_xcond_")}
    L1 = {k[9:]: v for k, v in n.items() if k.startswith("L1_xcond_")}
    parts = lambda v, k: np.split(v, k, axis=-1)
    ada, bada = parts(L0["w_ada"], 9), parts(L0["b_ada"], 9)
    wq, bq = parts(L1["Wss_q"], 2), parts(L1["bss_q"], 2)
    wk, bk = parts(L1["Wss_kv"], 2), parts(L1["bss_kv"], 2)
    bqkv, bkv0, bkv1, bm1 = parts(L0["b_qkv"], 3), parts(L0["b_kv"], 2), parts(L1["bkv"], 2), parts(L0["b_m1"], 2)
    flat = np.concatenate([bada[1], bada[4], bada[7], bq[0], bk[0], bada[0], bada[3], bada[6], bq[1], bk[1],
                           bqkv[0], bqkv[1], bqkv[2], L0["b_q"], bkv0[0], bkv0[1], L1["bq"], bkv1[0], bkv1[1],
                           bm1[0], bm1[1]])
    pair = np.arange(NCH)[None, :, None] * P + np.arange(P)[:, None, None]
    head = np.array(H0)[None, :, None] + np.arange(NHM)[None, None, :]
    return {
        "x": n["x"],
        "condT": np.ascontiguousarray(n["cond_1024"].T.reshape(KC, P, BATCH).transpose(1, 0, 2)),
        "ctxT": np.ascontiguousarray(n["ctx_1024"].transpose(2, 0, 1).reshape(KC, P, BATCH, LC).transpose(1, 0, 2, 3)),
        "ctxn": np.ascontiguousarray(n["ctx_1024"].transpose(1, 0, 2)),
        "cols": np.ascontiguousarray(flat.reshape(-1, P).T),
        "rows": np.stack([bada[2], bada[5], bada[8], L0["b_so"], L0["b_co"], L0["b_m2"], L1["bp"]])[None],
        "w_mod": _chunks(np.concatenate([ada[1], ada[4], ada[7], wq[0], wk[0], ada[0], ada[3], ada[6], wq[1], wk[1]], 1)),
        "w_gate": _chunks(np.concatenate([ada[2], ada[5], ada[8]], 1)),
        "w_qkv": _chunks(L0["w_qkv"]), "w_so": _chunks(L0["w_so"]), "w_q": _chunks(L0["w_q"]),
        "w_kv": _chunks(L0["w_kv"]), "w_co": _chunks(L0["w_co"]), "w_m1": _chunks(L0["w_m1"]),
        "w_m2": _chunks(L0["w_m2"]), "Wq": _chunks(L1["Wq"]), "Wkv": _chunks(L1["Wkv"]), "Wp": _chunks(L1["Wp"]),
        "ident": np.eye(P, dtype=np.float32),
        "mask4": (np.arange(P)[:, None] % 64 // HD == np.arange(4)[None, :]).astype(np.float32),
        "vmask": ((pair < PAIRS) & (pair // LC == head)).astype(np.float32),
    }


def kernel(**inputs):
    from concourse import bacc
    from concourse.bass_utils import run_bass_kernel_spmd

    nc = bacc.Bacc("TRN2", target_bir_lowering=False, num_devices=1)
    arrays, aps = {}, {}
    for name, arr in _laid_out(inputs).items():
        arrays[f"in_{name}"] = arr
        aps[name] = nc.dram_tensor(f"in_{name}", arr.shape, mybir.dt.from_np(arr.dtype), kind="ExternalInput").ap()
    out = nc.dram_tensor("out_0", (BATCH, LEN, CH), F32, kind="ExternalOutput").ap()
    block_kernel(nc, aps, out)
    r = run_bass_kernel_spmd(nc, [arrays], core_ids=[0])
    return r.results[0]["out_0"]
```

```python
from contextlib import ExitStack

import numpy as np
import concourse.bass as bass
from concourse import mybir

F32 = mybir.dt.float32
ALU = mybir.AluOpType
ACT = mybir.ActivationFunctionType
AX = mybir.AxisListType

BATCH, LEN, CH, HEADS, LC = 4, 1024, 256, 16, 77
P = 128
HD = CH // HEADS
KC = CH // P
HH = HEADS // KC
TPB = LEN // P
TILES = BATCH * TPB
SHIFT, TOPK, HID = 64, 16, 1024
HJ = HID // P
PAIRS = HEADS * LC
NCH = -(-PAIRS // P)
TAIL = PAIRS - (NCH - 1) * P
V1 = HD + 1
H0 = [P * c // LC for c in range(NCH)]
NH = [min(P * c + P - 1, PAIRS - 1) // LC - H0[c] + 1 for c in range(NCH)]
NHM = max(NH)
SCALE = 1.0 / float(HD) ** 0.5
LOW = -3.0e38
EPS0, EPS1 = 1e-6, 1e-5

COLS = [("mod_scale", 10), ("mod_shift", 10), ("bq_a", 2), ("bk_a", 2), ("bv_a", 2), ("bq_b", 2), ("bk_b", 2),
        ("bv_b", 2), ("bq_d", 2), ("bk_d", 2), ("bv_d", 2), ("bm1_a", HJ), ("bm1_b", HJ)]
COL = {}
for _name, _n in COLS:
    COL[_name] = sum(n for k, n in COLS[:len(COL)])
NCOLS = sum(n for _, n in COLS)


def block_kernel(nc, a, out):
    ctx = ExitStack()
    with ctx:
        def sb(name, shape, dt=F32, stack=ctx):
            return stack.enter_context(nc.sbuf_tensor(name, shape, dt))

        def sem(name):
            return ctx.enter_context(nc.semaphore(name))

        ps = ctx.enter_context(nc.psum_tensor("ps", [P, 8, 512], F32))
        PS = {s: ps[:, 2 * n:2 * n + 2, :] for n, s in enumerate("ABCD")}
        scratch = {s: nc.dram_tensor(f"v_flat_{s}", [BATCH, HEADS, LC, HD], F32, kind="Internal").ap() for s in "BD"}

        w_qkv = sb("w_qkv_sb", [P, KC, 3 * CH])
        w_so = sb("w_so_sb", [P, KC, CH])
        w_q = sb("w_q_sb", [P, KC, CH])
        w_co = sb("w_co_sb", [P, KC, CH])
        w_m1 = sb("w_m1_sb", [P, KC, 2 * HID])
        w_m2 = sb("w_m2_sb", [P, HJ, CH])
        w_qd = sb("w_qd_sb", [P, KC, CH])
        w_pd = sb("w_pd_sb", [P, KC, CH])
        cols = sb("cols_sb", [P, NCOLS])
        ident = sb("ident_sb", [P, P])
        mask4 = sb("mask4_sb", [P, 4])
        scaleT = sb("scaleT", [P, 10, BATCH])
        shiftT = sb("shiftT", [P, 10, BATCH])
        gate = sb("gate", [P, 3, BATCH, CH])
        gate_b = sb("gate_b", [P, 3, BATCH, CH])
        bp_row = sb("bp_row", [P, CH])
        kT = {s: sb(f"kT_{s}", [P, KC, BATCH, LC]) for s in "BD"}
        vblk = {s: sb(f"vblk_{s}", [P, BATCH, NCH, NHM * V1]) for s in "BD"}
        half_neg = sb("half_neg", [P, BATCH])

        eps = sb("eps", [P, 2])
        carrier = sb("carrier", [P, 1 + 4 + 4 * KC])

        X, XN, XG, HT, TMP, ST, MV, VE, RS = ({} for _ in range(9))

        def work(s):
            X[s] = sb(f"x_{s}", [P, CH])
            XN[s] = sb(f"xn_{s}", [P, CH])
            XG[s] = sb(f"xg_{s}", [P, CH])
            HT[s] = sb(f"hT_{s}", [P, KC, P])
            TMP[s] = sb(f"tmp_{s}", [P, CH])
            ST[s] = sb(f"st_{s}", [P, 6])
            MV[s] = sb(f"mv_{s}", [P, 2])
            VE[s] = sb(f"ve_{s}", [P, 1])
            RS[s] = sb(f"rstd_{s}", [P, 1])

        QT, KB, PR, PT, O, OT, MX, RC = ({} for _ in range(8))

        def attention_work(s, pairs):
            QT[s] = sb(f"qT_{s}", [P, KC, P])
            KB[s] = sb(f"kblk_{s}", [P, KC, 4, pairs])
            O[s] = sb(f"o_{s}", [P, HEADS, HD])
            OT[s] = sb(f"oT_{s}", [P, KC, P])
            MX[s] = sb(f"mx_{s}", [P, HEADS, 8])
            RC[s] = sb(f"rc_{s}", [P, HEADS, 1])
            if pairs == P:
                PR[s] = sb(f"p_{s}", [P, HEADS, P])
                PT[s] = sb(f"pT_{s}", [P, HEADS, P])
            else:
                PR[s] = sb(f"p_{s}", [P, NCH * P])
                PT[s] = sb(f"pT_{s}", [P, NCH, P])

        work("A")
        attention_work("A", P)
        kTa = sb("kT_A", [P, KC, P])
        va = sb("v_A", [P, HEADS, V1])

        with ExitStack() as early:
            w_mod = sb("w_mod_sb", [P, KC, 20 * P], F32, early)
            w_gate = sb("w_gate_sb", [P, KC, 3 * CH], F32, early)
            rows = sb("rows_sb", [P, 6, CH], F32, early)
            condT = sb("condT_sb", [P, KC, BATCH], F32, early)
            scT = sb("scT", [P, KC, BATCH], F32, early)
            screp = sb("screp", [P, KC, BATCH, P], F32, early)
            w_kv, vn, vf = {}, {}, {}

            def context_buffers(s):
                w_kv[s] = sb(f"w_kv_{s}_sb", [P, KC, 2 * CH], F32, early)
                vn[s] = sb(f"v_nat_{s}", [LC, BATCH, CH], F32, early)
                vf[s] = sb(f"v_flat_sb_{s}", [P, BATCH, NCH, V1], F32, early)

            ctxT = sb("ctxT_sb", [P, KC, BATCH, LC], F32, early)
            context_buffers("B")
            context_buffers("D")
            ctxn = sb("ctx_sb", [LC, BATCH, CH], F32, early)
            cn = sb("ctx_norm", [LC, BATCH, CH], F32, early)
            kvT = sb("kvT", [P, KC, BATCH, LC], F32, early)
            cst = sb("ctx_st", [LC, BATCH, 6], F32, early)
            cmv = sb("ctx_mv", [LC, BATCH, 2], F32, early)
            cve = sb("ctx_ve", [LC, BATCH], F32, early)
            crs = sb("ctx_rstd", [LC, BATCH], F32, early)
            vmask = sb("vmask_sb", [P, NCH, NHM], F32, early)

        work("B")
        attention_work("B", LC)
        S = sb("scores_B", [P, HEADS, LC])
        R = sb("scores_left_B", [P, HEADS, LC])
        MX2 = sb("mx2_B", [P, HEADS, 8])
        work("C")
        SA = sb("silu_C", [P, HJ, P])
        G = sb("hidden_C", [P, HJ, P])
        work("D")
        attention_work("D", LC)
        Y = sb("y_D", [P, CH])

        ld = {n: sem(f"ld_{n}") for n in ("cond", "small", "mod_a", "mod", "gate", "rows", "qkv", "so",
                                             "b", "kv_b", "kv_d", "c", "d", "ctx", "bp")}
        silu_done, rep_done = sem("silu_done"), sem("rep_done")
        mod_ps, mod_done, gate_ps, gate_done, gb_done = (sem(n) for n in (
            "mod_ps", "mod_done", "gate_ps", "gate_done", "gb_done"))
        zeroed, pad_ok = sem("zeroed"), {s: sem(f"pad_ok_{s}") for s in "BD"}
        cstat, crstd, cnorm, ct_ps, kv_hT = (sem(n) for n in ("cstat", "crstd", "cnorm", "ct_ps", "kv_hT"))
        ck_ps, ck_done, cv_ps, cv_done, v_out, v_in, vb_done = (
            {s: sem(f"{n}_{s}") for s in "BD"} for n in ("ck_ps", "ck_done", "cv_ps", "cv_done", "v_out", "v_in", "vb_done"))
        pool_self, dve_self = sem("pool_self"), sem("dve_self")

        def per_stage(name, stages="ABCD"):
            return {s: sem(f"{name}_{s}") for s in stages}

        x_in = per_stage("x_in")
        stats = per_stage("stats")
        rstd = per_stage("rstd")
        xn_ok = per_stage("xn_ok")
        xg_ok = per_stage("xg_ok")
        h_ps = per_stage("h_ps")
        h_ok = per_stage("h_ok")
        q_ps = per_stage("q_ps", "ABD")
        q_ok = per_stage("q_ok", "ABD")
        kb_ok = per_stage("kb_ok", "ABD")
        s_ps = per_stage("s_ps", "ABD")
        s_rd = per_stage("s_rd", "ABD")
        mx_ok = per_stage("mx_ok", "AD")
        p_ok = per_stage("p_ok", "ABD")
        pt_ps = per_stage("pt_ps", "ABD")
        pt_ok = per_stage("pt_ok", "ABD")
        pv_ps = per_stage("pv_ps", "ABD")
        rc_ok = per_stage("rc_ok", "ABD")
        o_ok = per_stage("o_ok", "ABD")
        ot_ps = per_stage("ot_ps", "ABD")
        ot_ok = per_stage("ot_ok", "ABD")
        y_ps = per_stage("y_ps")
        tmp_ok = per_stage("tmp_ok")
        top_ok = [sem(f"top_ok_{c}") for c in range(KC)]
        sm_ok = sem("sm_ok")
        e_ok = sem("e_ok")
        u_ps, sa_ok, g_ok = sem("u_ps"), sem("sa_ok"), sem("g_ok")
        y_out = sem("y_out")

        NEXT = {"A": "B", "B": "C", "C": "D"}
        LN = {"A": 0, "B": 1, "C": 2, "D": 3}
        EPS = {"A": EPS0, "B": EPS0, "C": EPS0, "D": EPS1}
        BQ = {"A": "bq_a", "B": "bq_b", "D": "bq_d"}
        BV = {"A": "bv_a", "B": "bv_b", "D": "bv_d"}
        GATE = {0: "C", 1: "B", 2: "C"}
        CV = {"B": "B", "D": "C"}
        WO = {"A": w_so, "B": w_co, "D": w_pd}

        def col(name, n=0):
            return cols[:, COL[name] + n:COL[name] + n + 1]

        def pick(view, t):
            b = t // TPB
            return view[:, b, :] if isinstance(b, int) else view[:, bass.ds(b, 1), :].rearrange("p b n -> p (b n)")

        def mod_col(table, idx, t):
            return pick(table[:, idx, :].rearrange("p (b n) -> p b n", n=1), t)

        DEPTH = 4

        def iterate(engine, body):
            for i in range(DEPTH + 1):
                body(i)
            with engine.Fori(DEPTH + 1, TILES) as i:
                body(i)
            for i in range(TILES, TILES + DEPTH):
                body(i)

        def run(step, s, i, lag, *more):
            t = i - lag
            if not isinstance(t, int) or 0 <= t < TILES:
                step(s, t, *more)

        def settle(dve, semaphore, value, slot):
            dve.wait_ge(semaphore, value)
            if not isinstance(value, int):
                nc.vector.tensor_copy(carrier[:, 1 + slot:2 + slot], carrier[:, 0:1])

        def starts(i, lag):
            return isinstance(i, int) and i == lag

        def first(t):
            return isinstance(t, int) and t == 0

        def pairs_view(ap, c):
            return ap[:, c * HH * LC:(c + 1) * HH * LC].rearrange("p (h k) -> p h k", h=HH)

        def score_banks(s, c=None):
            return PS[s][:, :, 0:4 * LC]

        block = ctx.enter_context(nc.Block())

        @block.sync
        def _(sp):
            def load_weights(dst, src, s):
                sp.dma_start(dst, src).then_inc(ld[s], 16)

            x_blocks = a["x"].rearrange("b (u p) c -> (b u) p c", p=SHIFT)
            out_blocks = out.rearrange("b (u p) c -> (b u) p c", p=SHIFT)
            PER = LEN // SHIFT

            def halves(t):
                second = (t // TPB) * PER + (2 * t + 2) % PER
                return 2 * t + 1, second

            def block_of(view, u):
                return view[u] if isinstance(u, int) else view[bass.ds(u, 1)].rearrange("a p c -> (a p) c")

            def load_x(t):
                if not first(t):
                    sp.wait_ge(xn_ok["A"], t)
                    sp.wait_ge(xg_ok["A"], t)
                for n, u in enumerate(halves(t)):
                    sp.dma_start(X["A"][n * SHIFT:(n + 1) * SHIFT, :], block_of(x_blocks, u)).then_inc(x_in["A"], 16)

            def store_y(t):
                sp.wait_ge(tmp_ok["D"], t + 1)
                for n, u in enumerate(halves(t)):
                    sp.dma_start(block_of(out_blocks, u), Y[n * SHIFT:(n + 1) * SHIFT, :]).then_inc(y_out, 16)

            load_weights(condT[:], a["condT"], "cond")
            load_weights(ident[:], a["ident"], "small")
            load_x(0)
            load_weights(w_mod[:, :, 0:4 * P], a["w_mod"][:, :, 0:4 * P], "mod_a")
            load_weights(cols[:], a["cols"], "small")
            load_weights(mask4[:], a["mask4"], "small")
            load_weights(w_qkv[:], a["w_qkv"], "qkv")
            for k in range(KC):
                load_weights(w_mod[:, k, 4 * P:20 * P], a["w_mod"][:, k, 4 * P:20 * P], "mod")
            load_weights(w_gate[:], a["w_gate"], "gate")
            load_weights(vmask[:], a["vmask"], "ctx")
            load_weights(ctxn[:], a["ctxn"], "ctx")
            load_weights(ctxT[:], a["ctxT"], "ctx")
            load_weights(rows[:], a["rows"][:, 0:6, :].partition_broadcast(P).rearrange("p a n c -> p (a n) c"), "rows")
            load_weights(w_kv["B"][:], a["w_kv"], "kv_b")
            load_weights(w_so[:], a["w_so"], "so")
            load_weights(w_kv["D"][:], a["Wkv"], "kv_d")
            load_weights(w_q[:], a["w_q"], "b")
            load_weights(w_co[:], a["w_co"], "b")
            load_weights(w_m1[:], a["w_m1"], "c")
            load_weights(w_m2[:], a["w_m2"], "c")
            load_weights(w_qd[:], a["Wq"], "d")
            load_weights(w_pd[:], a["Wp"], "d")
            load_weights(bp_row[:], a["rows"][:, 6, :].partition_broadcast(P).rearrange("p a c -> p (a c)"), "bp")

            def set_up_flat(s):
                sp.wait_ge(cv_done[s], 1)
                for b in range(BATCH):
                    sp.dma_start(scratch[s][b].rearrange("h k d -> k h d"),
                                 vn[s][:, b, :].rearrange("k (h d) -> k h d", h=HEADS)).then_inc(v_out[s], 16)
                sp.wait_ge(v_out[s], 16 * BATCH)
                sp.wait_ge(zeroed, 7)
                full = (NCH - 1) * P
                for b in range(BATCH):
                    flat = scratch[s][b].rearrange("h k d -> (h k) d")
                    sp.dma_start(vf[s][:, b, 0:NCH - 1, 0:HD],
                                 flat[0:full].rearrange("(c p) d -> p c d", p=P)).then_inc(v_in[s], 16)
                    sp.dma_start(vf[s][0:TAIL, b, NCH - 1, 0:HD], flat[full:PAIRS]).then_inc(v_in[s], 16)

            def load(s, t):
                if not first(t):
                    load_x(t)

            def store(s, t):
                store_y(t)

            def body(i):
                run(load, "A", i, 0)
                if isinstance(i, int) and i == 1:
                    set_up_flat("B")
                    set_up_flat("D")
                run(store, "D", i, 4)

            iterate(sp, body)
            sp.wait_ge(y_out, 32 * TILES)

        @block.gpsimd
        def _(pool):
            g = nc.gpsimd
            selfs = [0]

            def link(ins):
                selfs[0] += 1
                ins.then_inc(pool_self, 1)
                pool.wait_ge(pool_self, selfs[0])

            g.memset(half_neg[:], -0.5).then_inc(zeroed, 1)
            g.memset(va[:, :, HD:V1], 1.0).then_inc(zeroed, 1)
            for s in "BD":
                link(g.memset(vf[s][:], 0.0))
                g.memset(vf[s][:, :, :, HD:V1], 1.0).then_inc(zeroed, 1)
            g.memset(carrier[:], 0.0).then_inc(zeroed, 1)
            g.memset(eps[:, 0:1], EPS0).then_inc(zeroed, 1)
            g.memset(eps[:, 1:2], EPS1).then_inc(zeroed, 1)
            pool.wait_ge(zeroed, 7)

            def set_up_gates():
                pool.wait_ge(ld["rows"], 16)
                for n in range(3):
                    pool.wait_ge(gate_done, n + 1)
                    g.tensor_tensor(gate_b[:, n], gate[:, n], rows[:, 3 + n:4 + n, :].to_broadcast([P, BATCH, CH]),
                                    ALU.mult).then_inc(gb_done, 1)
                pool.wait_ge(gb_done, 3)
                g.memset(PR["B"][:, PAIRS:NCH * P], 0.0).then_inc(pad_ok["B"], 1)

            def set_up_context_rstd():
                pool.wait_ge(cstat, 2 * BATCH)
                link(g.tensor_scalar(cve[:], cmv[:, :, 1], EPS1, None, ALU.add))
                g.tensor_tensor(crs[:], cve[:], half_neg[0:LC, :], ALU.pow).then_inc(crstd, 1)

            def set_up_values(s):
                pool.wait_ge(v_in[s], 32 * BATCH)
                pool.wait_ge(ld["ctx"], 16 * 3)
                for b in range(BATCH):
                    ins = g.tensor_tensor(vblk[s][:, b].rearrange("p c (n v) -> p c n v", n=NHM),
                                          vf[s][:, b].unsqueeze(2).to_broadcast([P, NCH, NHM, V1]),
                                          vmask[:].unsqueeze(3).to_broadcast([P, NCH, NHM, V1]), ALU.mult)
                ins.then_inc(vb_done[s], 1)
                if s == "D":
                    g.memset(PR[s][:, PAIRS:NCH * P], 0.0).then_inc(pad_ok[s], 1)

            def reciprocal_root(s, t):
                pool.wait_ge(stats[s], 2 * t + 2)
                g.tensor_tensor(VE[s][:], MV[s][:, 1:2], eps[:, LN[s] // 3:LN[s] // 3 + 1], ALU.add).then_inc(rstd[s], 1)
                pool.wait_ge(rstd[s], 2 * t + 1)
                g.tensor_tensor(RS[s][:], VE[s][:], half_neg[:, 0:1], ALU.pow).then_inc(rstd[s], 1)

            def gated_bias(s, t):
                if s == "A":
                    pool.wait_ge(x_in[s], 32 * t + 32)
                if s != "D" and not first(t):
                    pool.wait_ge(x_in[NEXT[s]], t)
                if s == "D":
                    if not first(t):
                        pool.wait_ge(tmp_ok["D"], t)
                    else:
                        pool.wait_ge(ld["bp"], 16)
                    bias = bp_row[:]
                    pool.wait_ge(x_in[s], t + 1)
                else:
                    bias = pick(gate_b[:, LN[s]], t)
                    if s != "A":
                        pool.wait_ge(x_in[s], t + 1)
                g.tensor_tensor(XG[s][:], X[s][:], bias, ALU.add).then_inc(xg_ok[s], 1)

            def key_blocks(s, t):
                if first(t):
                    pool.wait_ge(ld["small"], 16 * 3)
                if s == "A":
                    pool.wait_ge(q_ok[s], t + 1)
                else:
                    pool.wait_ge(ck_done[s], 1)
                    if not first(t):
                        pool.wait_ge(s_ps[s], 2 * t)
                for c in range(KC):
                    if s == "A":
                        keys = kTa[:, c, :]
                        n = P
                    else:
                        keys = pick(kT[s][:, c], t)
                        n = LC
                    ins = g.tensor_tensor(KB[s][:, c], keys.unsqueeze(1).to_broadcast([P, 4, n]),
                                          mask4[:].unsqueeze(2).to_broadcast([P, 4, n]), ALU.mult)
                ins.then_inc(kb_ok[s], 1)

            def less_max(s, t, c):
                pool.wait_ge(top_ok[c], 4 * t + 1)
                g.tensor_tensor(pairs_view(PR["B"], c), S[:, c * HH:(c + 1) * HH, :],
                                MX["B"][:, c * HH:(c + 1) * HH, 0:1].to_broadcast([P, HH, LC]),
                                ALU.subtract).then_inc(sm_ok, 1)

            def residual(s, t):
                pool.wait_ge(tmp_ok[s], t + 1)
                nxt = NEXT[s]
                pool.wait_ge(xg_ok[s], t + 1)
                if not first(t):
                    pool.wait_ge(xn_ok[nxt], t)
                    pool.wait_ge(xg_ok[nxt], t)
                g.tensor_tensor(X[nxt][:], XG[s][:], TMP[s][:], ALU.add).then_inc(x_in[nxt], 1)

            def body(i):
                run(key_blocks, "B", i, 3)
                run(reciprocal_root, "A", i, 2)
                run(less_max, "B", i, 3, 0)
                if starts(i, 3):
                    set_up_values("B")
                run(gated_bias, "B", i, 3)
                run(less_max, "B", i, 3, 1)
                run(gated_bias, "C", i, 4)
                if starts(i, 4):
                    set_up_values("D")
                run(key_blocks, "A", i, 2)
                if starts(i, 2):
                    set_up_context_rstd()
                    set_up_gates()
                run(gated_bias, "A", i, 2)
                run(key_blocks, "D", i, 4)
                run(residual, "C", i, 4)
                run(reciprocal_root, "D", i, 4)
                run(residual, "B", i, 3)
                run(reciprocal_root, "C", i, 3)
                run(residual, "A", i, 2)
                run(reciprocal_root, "B", i, 2)
                run(gated_bias, "D", i, 4)

            iterate(pool, body)

        @block.scalar
        def _(act):
            sc = nc.scalar

            def set_up_keys(s):
                act.wait_ge(ck_ps[s], 1)
                for c in range(KC):
                    ins = sc.activation(kT[s][:, c].rearrange("p b k -> p (b k)"), PS["D"][:, c, 0:BATCH * LC],
                                        ACT.Identity, bias=col(f"bk_{s.lower()}", c))
                ins.then_inc(ck_done[s], 1)

            def set_up_values(s):
                act.wait_ge(cv_ps[s], 1)
                sc.copy(vn[s][:].rearrange("k (m n) c -> k m (n c)", m=2), PS[CV[s]][0:LC]).then_inc(cv_done[s], 1)

            def set_up_context():
                act.wait_ge(ct_ps, 1)
                act.wait_ge(mod_done, 5)
                for c in range(KC):
                    for b in range(BATCH):
                        ins = sc.activation(kvT[:, c, b, :], PS["C"][:, c, b * LC:(b + 1) * LC], ACT.Identity,
                                            scale=scaleT[:, 8 + c, b:b + 1], bias=shiftT[:, 8 + c, b:b + 1])
                ins.then_inc(kv_hT, 1)

            def modulate(s, t):
                act.wait_ge(h_ps[s], t + 1)
                if first(t):
                    act.wait_ge(mod_done, LN[s] + 1)
                for c in range(KC):
                    ins = sc.activation(HT[s][:, c, :], PS[s][:, 1, c * P:(c + 1) * P], ACT.Identity,
                                        scale=mod_col(scaleT, 2 * LN[s] + c, t), bias=mod_col(shiftT, 2 * LN[s] + c, t))
                ins.then_inc(h_ok[s], 1)

            def queries(s, t):
                act.wait_ge(q_ps[s], t + 1)
                for c in range(KC):
                    ins = sc.activation(QT[s][:, c, :], PS[s][:, 0, c * P:(c + 1) * P], ACT.Identity, bias=col(BQ[s], c))
                if s == "A":
                    for c in range(KC):
                        sc.activation(kTa[:, c, :], PS[s][:, 0, (KC + c) * P:(KC + c + 1) * P], ACT.Identity,
                                      bias=col("bk_a", c))
                    ins = sc.copy(va[:, :, 0:HD], PS[s][:, 1, CH:2 * CH].rearrange("p (h d) -> p h d", h=HEADS))
                ins.then_inc(q_ok[s], 1)

            def exponentials(s, t, c):
                if s == "A":
                    act.wait_ge(s_rd[s], 2 * t + c + 1)
                    w = PR[s][:, c * HH:(c + 1) * HH, :]
                    sc.activation(w, w, ACT.Exp, scale=SCALE).then_inc(p_ok[s], 1)
                elif s == "B":
                    act.wait_ge(sm_ok, 2 * t + c + 1)
                    w = pairs_view(PR[s], c)
                    sc.activation(w, w, ACT.Exp, scale=SCALE).then_inc(e_ok, 1)
                else:
                    act.wait_ge(s_rd[s], 2 * t + c + 1)
                    w = pairs_view(PR[s], c)
                    sc.activation(w, w, ACT.Exp, scale=SCALE).then_inc(p_ok[s], 1)

            def copy_scores(s, t, c):
                act.wait_ge(s_ps["B"], 2 * t + c + 1)
                sc.copy(S[:, c * HH:(c + 1) * HH, :].rearrange("p (j h) k -> p j (h k)", j=2),
                        score_banks("B")).then_inc(s_rd["B"], 1)

            def weights_out(s, t, c):
                act.wait_ge(pt_ps[s], 2 * t + c + 1)
                if s == "A":
                    ins = sc.copy(PT[s][:, c * HH:(c + 1) * HH, :].rearrange("p (j h) q -> p j (h q)", j=2), PS[s])
                elif c == 0:
                    ins = sc.copy(PT[s][:, 0:4, :].rearrange("p c q -> p (c q)"), PS[s][:, 0, :])
                else:
                    sc.copy(PT[s][:, 4:8, :].rearrange("p c q -> p (c q)"), PS[s][:, 1, :])
                    ins = sc.copy(PT[s][:, 8:NCH, :].rearrange("p c q -> p (c q)"), PS[s][:, 0, 0:(NCH - 8) * P])
                ins.then_inc(pt_ok[s], 1)

            def output_t(s, t):
                act.wait_ge(ot_ps[s], t + 1)
                for c in range(KC):
                    ins = sc.activation(OT[s][:, c, :], PS[s][:, 1, c * P:(c + 1) * P], ACT.Identity, bias=col(BV[s], c))
                ins.then_inc(ot_ok[s], 1)

            def silu(s, t, j):
                act.wait_ge(u_ps, HJ * t + j + 1)
                sc.activation(SA[:, j, :], PS["C"][:, j % 2, 0:P], ACT.Silu, bias=col("bm1_a", j)).then_inc(sa_ok, 1)

            def body(i):
                run(weights_out, "A", i, 1, 1)
                if starts(i, 1):
                    set_up_keys("B")
                run(queries, "D", i, 3)
                run(output_t, "B", i, 2)
                run(output_t, "A", i, 1)
                if starts(i, 1):
                    set_up_values("B")
                run(exponentials, "D", i, 3, 0)
                run(modulate, "C", i, 2)
                run(exponentials, "D", i, 3, 1)
                run(weights_out, "D", i, 3, 0)
                run(silu, "C", i, 2, 0)
                run(modulate, "B", i, 1)
                run(silu, "C", i, 2, 1)
                run(weights_out, "D", i, 3, 1)
                run(silu, "C", i, 2, 2)
                run(queries, "B", i, 1)
                if starts(i, 1):
                    set_up_context()
                run(silu, "C", i, 2, 3)
                run(copy_scores, "B", i, 1, 0)
                if starts(i, 1):
                    set_up_keys("D")
                run(modulate, "A", i, 0)
                run(silu, "C", i, 2, 4)
                run(copy_scores, "B", i, 1, 1)
                if starts(i, 1):
                    set_up_values("D")
                run(silu, "C", i, 2, 5)
                run(queries, "A", i, 0)
                run(silu, "C", i, 2, 6)
                run(silu, "C", i, 2, 7)
                run(exponentials, "B", i, 1, 0)
                run(exponentials, "B", i, 1, 1)
                run(exponentials, "A", i, 0, 0)
                run(weights_out, "B", i, 1, 0)
                run(output_t, "D", i, 3)
                run(weights_out, "B", i, 1, 1)
                run(exponentials, "A", i, 0, 1)
                run(weights_out, "A", i, 0, 0)
                run(modulate, "D", i, 2)

            act.wait_ge(ld["cond"], 16)
            sc.activation(scT[:], condT[:], ACT.Silu).then_inc(silu_done, 1)
            act.wait_ge(ld["small"], 16 * 3)
            iterate(act, body)

        @block.vector
        def _(dve):
            v = nc.vector

            def set_up_condition():
                dve.wait_ge(silu_done, 1)
                for c in range(KC):
                    ins = v.tensor_copy(screp[:, c], scT[:, c, :].unsqueeze(2).to_broadcast([P, BATCH, P]))
                ins.then_inc(rep_done, 1)

            def set_up_context_statistics():
                dve.wait_ge(ld["ctx"], 16 * 3)
                for b in range(BATCH):
                    v.bn_stats(cst[:, b, :], ctxn[:, b, :]).then_inc(cstat, 1)
                dve.wait_ge(cstat, BATCH)
                for b in range(BATCH):
                    v.bn_aggr(cmv[:, b, :], cst[:, b, :]).then_inc(cstat, 1)

            def set_up_context():
                dve.wait_ge(crstd, 1)
                for b in range(BATCH):
                    ins = v.tensor_scalar(cn[:, b, :], ctxn[:, b, :], cmv[:, b, 0:1], crs[:, b:b + 1],
                                          ALU.subtract, ALU.mult)
                ins.then_inc(cnorm, 1)

            def set_up_modulation(ln):
                dve.wait_ge(mod_ps, ln + 1)
                if ln == 0:
                    dve.wait_ge(ld["small"], 16 * 3)
                mod = PS["D"][:, ln % 2, 0:16].rearrange("p (m i b) -> p m i b", m=2, b=BATCH)
                for m, (table, name) in enumerate(((scaleT, "mod_scale"), (shiftT, "mod_shift"))):
                    ins = v.scalar_tensor_tensor(
                        out=table[:, 2 * ln:2 * ln + 2, :], in0=mod[:, m], scalar=1.0 - m,
                        in1=cols[:, COL[name] + 2 * ln:COL[name] + 2 * ln + 2].unsqueeze(2).to_broadcast([P, KC, BATCH]),
                        op0=ALU.add, op1=ALU.add)
                ins.then_inc(mod_done, 1)

            def set_up_gate(n):
                dve.wait_ge(gate_ps, n + 1)
                if n == 0:
                    dve.wait_ge(ld["rows"], 16)
                v.tensor_tensor(gate[:, n].rearrange("p (m b) c -> p m b c", m=2),
                                PS[GATE[n]].rearrange("p m (b c) -> p m b c", b=2),
                                rows[:, n:n + 1, :].unsqueeze(1).to_broadcast([P, 2, 2, CH]), ALU.add).then_inc(gate_done, 1)

            def statistics(s, t):
                dve.wait_ge(x_in[s], 32 * t + 32 if s == "A" else t + 1)
                v.bn_stats(ST[s][:], X[s][:]).then_inc(stats[s], 1)
                if not first(t):
                    dve.wait_ge(xn_ok[s], t)
                settle(dve, stats[s], 2 * t + 1, LN[s])
                v.bn_aggr(MV[s][:], ST[s][:]).then_inc(stats[s], 1)

            def normalise(s, t):
                dve.wait_ge(rstd[s], 2 * t + 2)
                if not first(t):
                    dve.wait_ge(h_ps[s], t)
                v.tensor_scalar(XN[s][:], X[s][:], MV[s][:, 0:1], RS[s][:], ALU.subtract, ALU.mult).then_inc(xn_ok[s], 1)

            def maxima(s, t, c):
                dve.wait_ge(s_ps[s], 2 * t + c + 1)
                view = (PS[s].rearrange("p j (h k) -> p j h k", h=4) if s == "A"
                        else score_banks(s).rearrange("p j (h k) -> p j h k", h=4))
                v.tensor_reduce(MX[s][:, c * HH:(c + 1) * HH, 0].rearrange("p (j h) -> p j h", j=2), view,
                                AX.X, ALU.max).then_inc(mx_ok[s], 1)
                dve.wait_ge(mx_ok[s], 2 * t + c + 1)
                w = PR[s][:, c * HH:(c + 1) * HH, :] if s == "A" else pairs_view(PR[s], c)
                n = P if s == "A" else LC
                v.tensor_tensor(w.rearrange("p (j h) k -> p j h k", j=2), view,
                                MX[s][:, c * HH:(c + 1) * HH, 0:1].rearrange("p (j h) o -> p j h o", j=2)
                                .to_broadcast([P, 2, 4, n]), ALU.subtract).then_inc(s_rd[s], 1)

            def select(s, t, c, step):
                if step == 0:
                    settle(dve, s_rd["B"], 2 * t + c + 1, 4 + 4 * c)
                else:
                    settle(dve, top_ok[c], 4 * t + step, 4 + 4 * c + step)
                for h in range(c * HH, (c + 1) * HH):
                    if step == 0:
                        ins = v.max(MX["B"][:, h, :], S[:, h, :])
                    elif step == 1:
                        ins = v.match_replace(R[:, h, :], MX["B"][:, h, :], S[:, h, :], LOW)
                    elif step == 2:
                        ins = v.max(MX2[:, h, :], R[:, h, :])
                    else:
                        ins = v.match_replace(R[:, h, :], MX2[:, h, :], R[:, h, :], LOW)
                ins.then_inc(top_ok[c], 1)

            def keep_chosen(s, t, c):
                dve.wait_ge(top_ok[c], 4 * t + 4)
                dve.wait_ge(e_ok, 2 * t + c + 1)
                w = PR["B"][:, c * HH * LC:(c + 1) * HH * LC]
                v.scalar_tensor_tensor(out=w, in0=R[:, c * HH:(c + 1) * HH, :].rearrange("p h k -> p (h k)"), scalar=LOW,
                                       in1=w, op0=ALU.is_equal, op1=ALU.mult).then_inc(p_ok["B"], 1)

            def normalise_output(s, t):
                dve.wait_ge(pv_ps[s], t + 1)
                acc = PS[s][:, 0, 0:HEADS * V1].rearrange("p (h v) -> p h v", h=HEADS)
                v.reciprocal(RC[s][:], acc[:, :, HD:V1]).then_inc(rc_ok[s], 1)
                dve.wait_ge(rc_ok[s], t + 1)
                v.tensor_tensor(O[s][:], acc[:, :, 0:HD], RC[s][:].to_broadcast([P, HEADS, HD]),
                                ALU.mult).then_inc(o_ok[s], 1)

            def gated(s, t):
                dve.wait_ge(y_ps[s], t + 1)
                y = PS[s][:, 0, 0:CH]
                if s == "D":
                    dve.wait_ge(xg_ok[s], t + 1)
                    if not first(t):
                        dve.wait_ge(y_out, 32 * t)
                    v.tensor_tensor(Y[:], y, XG[s][:], ALU.add).then_inc(tmp_ok[s], 1)
                    return
                if first(t):
                    dve.wait_ge(gate_done, LN[s] + 1)
                else:
                    dve.wait_ge(x_in[NEXT[s]], t)
                v.tensor_tensor(TMP[s][:], y, pick(gate[:, LN[s]], t), ALU.mult).then_inc(tmp_ok[s], 1)

            def hidden(s, t, j):
                dve.wait_ge(sa_ok, HJ * t + j + 1)
                v.scalar_tensor_tensor(out=G[:, j, :], in0=PS["C"][:, j % 2, P:2 * P], scalar=col("bm1_b", j),
                                       in1=SA[:, j, :], op0=ALU.add, op1=ALU.mult).then_inc(g_ok, 1)

            def body(i):
                run(maxima, "A", i, 1, 1)
                if starts(i, 1):
                    set_up_gate(1)
                    set_up_modulation(4)
                    set_up_gate(2)
                    set_up_context()
                run(statistics, "D", i, 3)
                run(normalise, "D", i, 3)
                run(normalise_output, "B", i, 2)
                run(gated, "D", i, 4)
                run(maxima, "D", i, 3, 0)
                run(gated, "B", i, 2)
                run(statistics, "C", i, 2)
                run(normalise_output, "A", i, 1)
                run(normalise, "C", i, 2)
                run(maxima, "D", i, 3, 1)
                run(gated, "A", i, 1)
                run(statistics, "B", i, 1)
                run(normalise, "B", i, 1)
                run(hidden, "C", i, 2, 0)
                run(hidden, "C", i, 2, 1)
                run(statistics, "A", i, 0)
                if starts(i, 0):
                    set_up_condition()
                run(hidden, "C", i, 2, 2)
                run(normalise, "A", i, 0)
                if starts(i, 0):
                    set_up_modulation(0)
                    set_up_modulation(1)
                    set_up_modulation(2)
                run(hidden, "C", i, 2, 3)
                run(select, "B", i, 1, 0, 0)
                run(select, "B", i, 1, 0, 1)
                run(hidden, "C", i, 2, 4)
                run(select, "B", i, 1, 1, 0)
                run(select, "B", i, 1, 0, 2)
                run(hidden, "C", i, 2, 5)
                run(select, "B", i, 1, 1, 1)
                run(hidden, "C", i, 2, 6)
                run(select, "B", i, 1, 0, 3)
                run(hidden, "C", i, 2, 7)
                run(select, "B", i, 1, 1, 2)
                run(keep_chosen, "B", i, 1, 0)
                run(maxima, "A", i, 0, 0)
                if starts(i, 0):
                    set_up_context_statistics()
                    set_up_modulation(3)
                    set_up_gate(0)
                run(select, "B", i, 1, 1, 3)
                run(normalise_output, "D", i, 3)
                run(keep_chosen, "B", i, 1, 1)
                run(gated, "C", i, 2)

            dve.wait_ge(zeroed, 7)
            iterate(dve, body)

        @block.tensor
        def _(pe):
            mm = nc.tensor.matmul

            def set_up_modulation(ln):
                if ln == 0:
                    pe.wait_ge(silu_done, 1)
                    pe.wait_ge(ld["mod_a"], 16)
                elif ln == 1:
                    pe.wait_ge(ld["mod"], 32)
                if ln >= 2:
                    pe.wait_ge(mod_done, ln - 1)
                for i in range(4 * ln, 4 * ln + 4):
                    for c in range(KC):
                        ins = mm(PS["D"][:, ln % 2, i % 4 * BATCH:(i % 4 + 1) * BATCH], w_mod[:, c, i * P:(i + 1) * P], scT[:, c, :],
                                 start=(c == 0), stop=(c == KC - 1))
                ins.then_inc(mod_ps, 1)

            def set_up_gate(n):
                if n == 0:
                    pe.wait_ge(rep_done, 1)
                    pe.wait_ge(ld["gate"], 16)
                if n == 2:
                    pe.wait_ge(gate_done, 1)
                for b in range(BATCH):
                    for c in range(KC):
                        ins = mm(PS[GATE[n]][:, b // 2, (b % 2) * CH:(b % 2 + 1) * CH], screp[:, c, b, :],
                                 w_gate[:, c, n * CH:(n + 1) * CH], start=(c == 0), stop=(c == KC - 1))
                ins.then_inc(gate_ps, 1)

            def set_up_keys(s):
                if s == "B":
                    pe.wait_ge(mod_done, 5)
                    pe.wait_ge(ld["ctx"], 16 * 3)
                    pe.wait_ge(ld["kv_b"], 16)
                else:
                    pe.wait_ge(ck_done["B"], 1)
                    pe.wait_ge(kv_hT, 1)
                    pe.wait_ge(ld["kv_d"], 16)
                src = ctxT if s == "B" else kvT
                for c in range(KC):
                    for k in range(KC):
                        ins = mm(PS["D"][:, c, 0:BATCH * LC], w_kv[s][:, k, c * P:(c + 1) * P],
                                 src[:, k].rearrange("p b k -> p (b k)"), start=(k == 0), stop=(k == KC - 1))
                ins.then_inc(ck_ps[s], 1)

            def set_up_values(s):
                if s == "B":
                    pe.wait_ge(gate_done, 2)
                else:
                    pe.wait_ge(kv_hT, 1)
                src = ctxT if s == "B" else kvT
                for b in range(BATCH):
                    for k in range(KC):
                        ins = mm(PS[CV[s]][0:LC, b // 2, (b % 2) * CH:(b % 2 + 1) * CH], src[:, k, b, :],
                                 w_kv[s][:, k, CH:2 * CH], start=(k == 0), stop=(k == KC - 1))
                ins.then_inc(cv_ps[s], 1)

            def set_up_context():
                pe.wait_ge(gate_done, 3)
                pe.wait_ge(cnorm, 1)
                for c in range(KC):
                    for b in range(BATCH):
                        ins = nc.tensor.transpose(PS["C"][:, c, b * LC:(b + 1) * LC], cn[:, b, c * P:(c + 1) * P],
                                                  ident[0:LC, 0:LC])
                ins.then_inc(ct_ps, 1)

            def transpose_h(s, t):
                pe.wait_ge(xn_ok[s], t + 1)
                if first(t):
                    if s == "A":
                        pe.wait_ge(ld["small"], 16 * 3)
                    elif s == "B":
                        pe.wait_ge(cv_done["B"], 1)
                    elif s == "C":
                        pe.wait_ge(cv_done["D"], 1)
                    else:
                        pe.wait_ge(ck_done["D"], 1)
                for c in range(KC):
                    ins = nc.tensor.transpose(PS[s][:, 1, c * P:(c + 1) * P], XN[s][:, c * P:(c + 1) * P], ident[:])
                ins.then_inc(h_ps[s], 1)

            def project_q(s, t):
                pe.wait_ge(h_ok[s], t + 1)
                if first(t):
                    pe.wait_ge(ld[{"A": "qkv", "B": "b", "D": "d"}[s]], 32 if s != "A" else 16)
                else:
                    pe.wait_ge(tmp_ok[s], t)
                w = {"A": w_qkv, "B": w_q, "D": w_qd}[s]
                for c in range(4 if s == "A" else 2):
                    for k in range(KC):
                        ins = mm(PS[s][:, 0, c * P:(c + 1) * P], w[:, k, c * P:(c + 1) * P], HT[s][:, k, :],
                                 start=(k == 0), stop=(k == KC - 1))
                if s == "A":
                    for k in range(KC):
                        ins = mm(PS[s][:, 1, CH:2 * CH], HT[s][:, k, :], w[:, k, 2 * CH:3 * CH],
                                 start=(k == 0), stop=(k == KC - 1))
                ins.then_inc(q_ps[s], 1)

            def scores(s, t, c):
                if c == 0:
                    pe.wait_ge(q_ok[s], t + 1)
                    pe.wait_ge(kb_ok[s], t + 1)
                else:
                    pe.wait_ge(s_rd[s], 2 * t + 1)
                n = 4 * (P if s == "A" else LC)
                for j in range(2):
                    rows_ = slice(64 * j, 64 * j + 64)
                    ins = mm(PS[s][:, j, 0:n], QT[s][rows_, c, :], KB[s][rows_, c].rearrange("p h k -> p (h k)"),
                             start=True, stop=True)
                ins.then_inc(s_ps[s], 1)

            def transpose_p(s, t, c):
                if c == 0:
                    pe.wait_ge(s_rd[s], 2 * t + 2)
                    if s != "A" and first(t):
                        pe.wait_ge(pad_ok[s], 1)
                else:
                    pe.wait_ge(pt_ok[s], 2 * t + 1)
                pe.wait_ge(p_ok[s], 2 * t + c + 1)
                if s == "A":
                    for h in range(HH):
                        ins = nc.tensor.transpose(PS[s][:, h // 4, (h % 4) * P:(h % 4 + 1) * P],
                                                  PR[s][:, c * HH + h, :], ident[:])
                else:
                    for n in (range(4) if c == 0 else range(4, NCH)):
                        bank = 1 if 4 <= n < 8 else 0
                        ins = nc.tensor.transpose(PS[s][:, bank, (n % 4) * P:(n % 4 + 1) * P],
                                                  PR[s][:, n * P:(n + 1) * P], ident[:])
                ins.then_inc(pt_ps[s], 1)

            def weigh_values(s, t, part, parts):
                if part == 0:
                    pe.wait_ge(pt_ok[s], 2 * t + 2)
                if s == "A":
                    for h in range(part * HEADS // parts, (part + 1) * HEADS // parts):
                        ins = mm(PS[s][:, 0, h * V1:(h + 1) * V1], PT[s][:, h, :], va[:, h, :], start=True, stop=True)
                else:
                    if first(t) and part == 0:
                        pe.wait_ge(vb_done[s], 1)
                    for n in range(part * NCH // parts, (part + 1) * NCH // parts):
                        ins = mm(PS[s][:, 0, H0[n] * V1:(H0[n] + NH[n]) * V1], PT[s][:, n, :],
                                 pick(vblk[s][:, :, n, 0:NH[n] * V1], t), start=(n == 0), stop=(n == NCH - 1),
                                 skip_group_check=True)
                if part == parts - 1:
                    ins.then_inc(pv_ps[s], 1)

            def transpose_o(s, t):
                pe.wait_ge(o_ok[s], t + 1)
                for c in range(KC):
                    ins = nc.tensor.transpose(PS[s][:, 1, c * P:(c + 1) * P],
                                              O[s][:].rearrange("p h d -> p (h d)")[:, c * P:(c + 1) * P], ident[:])
                ins.then_inc(ot_ps[s], 1)

            def project_o(s, t):
                pe.wait_ge(ot_ok[s], t + 1)
                if first(t) and s == "A":
                    pe.wait_ge(ld["so"], 16)
                for k in range(KC):
                    ins = mm(PS[s][:, 0, 0:CH], OT[s][:, k, :], WO[s][:, k, :], start=(k == 0), stop=(k == KC - 1))
                ins.then_inc(y_ps[s], 1)

            def up(s, t, j):
                if j == 0:
                    pe.wait_ge(h_ok["C"], t + 1)
                    if first(t):
                        pe.wait_ge(ld["c"], 32)
                    else:
                        pe.wait_ge(tmp_ok["C"], t)
                elif j >= 2:
                    pe.wait_ge(g_ok, HJ * t + j - 1)
                for half in range(2):
                    for k in range(KC):
                        m = half * HID + j * P
                        ins = mm(PS["C"][:, j % 2, half * P:(half + 1) * P], w_m1[:, k, m:m + P], HT["C"][:, k, :],
                                 start=(k == 0), stop=(k == KC - 1))
                ins.then_inc(u_ps, 1)

            def down(s, t, half):
                if half == 0:
                    pe.wait_ge(g_ok, HJ * t + HJ)
                for j in range(half * HJ // 2, (half + 1) * HJ // 2):
                    ins = mm(PS["C"][:, 0, 0:CH], G[:, j, :], w_m2[:, j, :], start=(j == 0), stop=(j == HJ - 1))
                if half == 1:
                    ins.then_inc(y_ps["C"], 1)

            def body(i):
                run(transpose_h, "A", i, 0)
                if starts(i, 0):
                    set_up_modulation(0)
                run(up, "C", i, 2, 5)
                run(scores, "B", i, 1, 1)
                if starts(i, 1):
                    set_up_values("D")
                run(project_q, "A", i, 0)
                if starts(i, 0):
                    set_up_modulation(1)
                    set_up_modulation(2)
                run(up, "C", i, 2, 6)
                run(weigh_values, "D", i, 3, 0, 2)
                run(up, "C", i, 2, 7)
                run(weigh_values, "D", i, 3, 1, 2)
                run(scores, "A", i, 0, 0)
                if starts(i, 0):
                    set_up_modulation(3)
                    set_up_gate(0)
                run(down, "C", i, 2, 0)
                run(transpose_p, "B", i, 1, 0)
                run(down, "C", i, 2, 1)
                run(scores, "A", i, 0, 1)
                if starts(i, 0):
                    set_up_gate(1)
                    set_up_modulation(4)
                run(transpose_o, "D", i, 3)
                run(transpose_p, "B", i, 1, 1)
                run(project_o, "D", i, 3)
                run(weigh_values, "B", i, 1, 0, 2)
                run(transpose_p, "A", i, 0, 0)
                if starts(i, 0):
                    set_up_gate(2)
                run(weigh_values, "B", i, 1, 1, 2)
                run(transpose_h, "D", i, 2)
                run(transpose_p, "A", i, 0, 1)
                if starts(i, 0):
                    set_up_keys("B")
                run(transpose_o, "B", i, 1)
                run(project_q, "D", i, 2)
                run(weigh_values, "A", i, 0, 0, 4)
                run(scores, "D", i, 2, 0)
                run(project_o, "B", i, 1)
                run(weigh_values, "A", i, 0, 1, 4)
                run(weigh_values, "A", i, 0, 2, 4)
                run(weigh_values, "A", i, 0, 3, 4)
                if starts(i, 0):
                    set_up_context()
                run(scores, "D", i, 2, 1)
                run(transpose_o, "A", i, 0)
                run(transpose_h, "C", i, 1)
                run(project_o, "A", i, 0)
                if starts(i, 0):
                    set_up_values("B")
                run(transpose_p, "D", i, 2, 0)
                run(up, "C", i, 1, 0)
                run(up, "C", i, 1, 1)
                run(transpose_p, "D", i, 2, 1)
                run(transpose_h, "B", i, 0)
                run(up, "C", i, 1, 2)
                run(project_q, "B", i, 0)
                run(up, "C", i, 1, 3)
                run(scores, "B", i, 0, 0)
                if starts(i, 0):
                    set_up_keys("D")
                run(up, "C", i, 1, 4)

            iterate(pe, body)


def _chunks(w):
    return np.ascontiguousarray(w.reshape(-1, P, w.shape[-1]).transpose(1, 0, 2))


def _laid_out(i):
    n = {k: np.asarray(v) for k, v in i.items()}
    L0 = {k[9:]: v for k, v in n.items() if k.startswith("L0_xcond_")}
    L1 = {k[9:]: v for k, v in n.items() if k.startswith("L1_xcond_")}
    parts = lambda v, k: np.split(v, k, axis=-1)
    ada, bada = parts(L0["w_ada"], 9), parts(L0["b_ada"], 9)
    wq, bq = parts(L1["Wss_q"], 2), parts(L1["bss_q"], 2)
    wk, bk = parts(L1["Wss_kv"], 2), parts(L1["bss_kv"], 2)
    bqkv, bkv0, bkv1, bm1 = parts(L0["b_qkv"], 3), parts(L0["b_kv"], 2), parts(L1["bkv"], 2), parts(L0["b_m1"], 2)
    flat = np.concatenate([bada[1], bada[4], bada[7], bq[0], bk[0], bada[0], bada[3], bada[6], bq[1], bk[1],
                           bqkv[0], bqkv[1], bqkv[2], L0["b_q"], bkv0[0], bkv0[1], L1["bq"], bkv1[0], bkv1[1],
                           bm1[0], bm1[1]])
    pair = np.arange(NCH)[None, :, None] * P + np.arange(P)[:, None, None]
    head = np.array(H0)[None, :, None] + np.arange(NHM)[None, None, :]
    return {
        "x": n["x"],
        "condT": np.ascontiguousarray(n["cond_1024"].T.reshape(KC, P, BATCH).transpose(1, 0, 2)),
        "ctxT": np.ascontiguousarray(n["ctx_1024"].transpose(2, 0, 1).reshape(KC, P, BATCH, LC).transpose(1, 0, 2, 3)),
        "ctxn": np.ascontiguousarray(n["ctx_1024"].transpose(1, 0, 2)),
        "cols": np.ascontiguousarray(flat.reshape(-1, P).T),
        "rows": np.stack([bada[2], bada[5], bada[8], L0["b_so"], L0["b_co"], L0["b_m2"], L1["bp"]])[None],
        "w_mod": _chunks(np.concatenate([ada[1], ada[0], ada[4], ada[3], ada[7], ada[6], wq[0], wq[1], wk[0], wk[1]], 1)),
        "w_gate": _chunks(np.concatenate([ada[2], ada[5], ada[8]], 1)),
        "w_qkv": _chunks(L0["w_qkv"]), "w_so": _chunks(L0["w_so"]), "w_q": _chunks(L0["w_q"]),
        "w_kv": _chunks(L0["w_kv"]), "w_co": _chunks(L0["w_co"]), "w_m1": _chunks(L0["w_m1"]),
        "w_m2": _chunks(L0["w_m2"]), "Wq": _chunks(L1["Wq"]), "Wkv": _chunks(L1["Wkv"]), "Wp": _chunks(L1["Wp"]),
        "ident": np.eye(P, dtype=np.float32),
        "mask4": (np.arange(P)[:, None] % 64 // HD == np.arange(4)[None, :]).astype(np.float32),
        "vmask": ((pair < PAIRS) & (pair // LC == head)).astype(np.float32),
    }


def kernel(**inputs):
    from concourse import bacc
    from concourse.bass_utils import run_bass_kernel_spmd

    nc = bacc.Bacc("TRN2", target_bir_lowering=False, num_devices=1)
    arrays, aps = {}, {}
    for name, arr in _laid_out(inputs).items():
        arrays[f"in_{name}"] = arr
        aps[name] = nc.dram_tensor(f"in_{name}", arr.shape, mybir.dt.from_np(arr.dtype), kind="ExternalInput").ap()
    out = nc.dram_tensor("out_0", (BATCH, LEN, CH), F32, kind="ExternalOutput").ap()
    block_kernel(nc, aps, out)
    r = run_bass_kernel_spmd(nc, [arrays], core_ids=[0])
    return r.results[0]["out_0"]
```
